# Optimizing a Trainium2 kernel written in Bass

```python
import numpy as np
import jax
import jax.numpy as jnp

def _softmax(x, axis=-1):
    return jax.nn.softmax(x, axis=axis)

def _gelu(x):
    return jax.nn.gelu(x, approximate=True)

def _silu(x):
    return jax.nn.silu(x)

def _sigmoid(x):
    return jax.nn.sigmoid(x)

def _layernorm(x, axis=-1, eps=1e-05):
    m = jnp.mean(x, axis=axis, keepdims=True)
    v = jnp.var(x, axis=axis, keepdims=True)
    return (x - m) / jnp.sqrt(v + eps)

def _scatter_add(tgt, idx, src, axis=0):
    return tgt.at[idx].add(src)

def _segment_sum(src, seg, n):
    return jax.ops.segment_sum(src, seg, n)
kernel_name = 'mk_xattn_ffn_d1_seqx_r4_d457e2'

def setup_inputs(seed: int=0):
    np.random.seed(seed)
    _w = jnp.asarray

    def _rec_inputs():
        import jax
        import jax.numpy as jnp
        _rk = jax.random.key(seed)
        x = 7.22e-05 + 1 * jax.random.normal(jax.random.fold_in(_rk, 1), (4, 512, 512), jnp.float32)
        _lenS = 512 - jax.random.randint(jax.random.fold_in(_rk, 7), (4,), 0, max(1, 512 // 4) + 1, jnp.int32)
        _lenS2 = 512 - jax.random.randint(jax.random.fold_in(_rk, 8), (4,), 0, max(1, 512 // 4) + 1, jnp.int32)
        _ctx_1024P = jax.random.normal(jax.random.fold_in(_rk, 11), (4, 16, 256), jnp.float32)
        _ctx_1024c = jax.random.dirichlet(jax.random.fold_in(_rk, 511), 0.3 * jnp.ones((16,), jnp.float32), (4, 512))
        _ctx_1024t = jnp.einsum('bsk,bkd->bsd', _ctx_1024c, _ctx_1024P)
        _ctx_1024t = _ctx_1024t * jax.lax.rsqrt(jnp.mean(jnp.square(_ctx_1024t)) + 1e-12) * 0.953939
        ctx_1024 = 2.81802e-05 + 1.00001 * (_ctx_1024t + 0.3 * jax.random.normal(jax.random.fold_in(_rk, 611), (4, 512, 256), jnp.float32))
        return (x, ctx_1024)
    x, ctx_1024 = _rec_inputs()

    def _L0_xattn_setup():
        import jax, jax.numpy as jnp
        import numpy as np
        key = jax.random.key(seed)
        ks = jax.random.split(key, 6)
        B, L, N, C, D = (8, 128, 512, 256, 128)
        return {'teacher_logits': jax.random.normal(ks[0], (B, L, N), dtype=jnp.float32), 'teacher_features': jax.random.normal(ks[1], (B, N, C), dtype=jnp.float32), 'Wq': jax.random.normal(ks[2], (D, C), dtype=jnp.float32) * (1.0 / np.sqrt(C)), 'bq': jnp.zeros((D,), dtype=jnp.float32), 'Wk': jax.random.normal(ks[3], (D, C), dtype=jnp.float32) * (1.0 / np.sqrt(C)), 'bk': jnp.zeros((D,), dtype=jnp.float32)}
    _L0_xattn_all = _L0_xattn_setup()
    _L0_xattn_in = {k: v for k, v in _L0_xattn_all.items() if k in ('Wq', 'bq', 'Wk', 'bk')}
    del _L0_xattn_all

    def _L0_ffn_setup():
        import jax, jax.numpy as jnp
        import numpy as np
        B, S, H = (2, 256, 512)
        E, K = (8, 2)
        I = 352
        IS = 1408
        WSCALE = 0.02
        key = jax.random.key(seed)
        ks = jax.random.split(key, 9)
        f32 = jnp.float32
        return {'hidden_states': jax.random.normal(ks[0], (B, S, H), dtype=f32), 'gate_w': jax.random.normal(ks[1], (E, H), dtype=f32) * WSCALE, 'w_gate': jax.random.normal(ks[2], (E, H, I), dtype=f32) * WSCALE, 'w_up': jax.random.normal(ks[3], (E, H, I), dtype=f32) * WSCALE, 'w_down': jax.random.normal(ks[4], (E, I, H), dtype=f32) * WSCALE, 'sw_gate': jax.random.normal(ks[5], (H, IS), dtype=f32) * WSCALE, 'sw_up': jax.random.normal(ks[6], (H, IS), dtype=f32) * WSCALE, 'sw_down': jax.random.normal(ks[7], (IS, H), dtype=f32) * WSCALE, 'shared_gate_w': jax.random.normal(ks[8], (H, 1), dtype=f32) * WSCALE}
    _L0_ffn_all = _L0_ffn_setup()
    _L0_ffn_in = {k: v for k, v in _L0_ffn_all.items() if k in ('gate_w', 'w_gate', 'w_up', 'w_down', 'sw_gate', 'sw_up', 'sw_down', 'shared_gate_w')}
    del _L0_ffn_all
    return {'x': x, 'ctx_1024': ctx_1024, 'L0_xattn_Wq': _L0_xattn_in['Wq'], 'L0_xattn_bq': _L0_xattn_in['bq'], 'L0_xattn_Wk': _L0_xattn_in['Wk'], 'L0_xattn_bk': _L0_xattn_in['bk'], 'L0_ffn_gate_w': _L0_ffn_in['gate_w'], 'L0_ffn_w_gate': _L0_ffn_in['w_gate'], 'L0_ffn_w_up': _L0_ffn_in['w_up'], 'L0_ffn_w_down': _L0_ffn_in['w_down'], 'L0_ffn_sw_gate': _L0_ffn_in['sw_gate'], 'L0_ffn_sw_up': _L0_ffn_in['sw_up'], 'L0_ffn_sw_down': _L0_ffn_in['sw_down'], 'L0_ffn_shared_gate_w': _L0_ffn_in['shared_gate_w']}

def reference(x, ctx_1024, L0_xattn_Wq, L0_xattn_bq, L0_xattn_Wk, L0_xattn_bk, L0_ffn_gate_w, L0_ffn_w_gate, L0_ffn_w_up, L0_ffn_w_down, L0_ffn_sw_gate, L0_ffn_sw_up, L0_ffn_sw_down, L0_ffn_shared_gate_w):
    import jax
    import jax.numpy as jnp

    def _L0_xattn_ref(teacher_logits, teacher_features, Wq, bq, Wk, bk):
        import jax, jax.numpy as jnp
        import numpy as np
        query = jnp.einsum('bnc,dc->bnd', teacher_features, Wq) + bq
        key = jnp.einsum('bnc,dc->bnd', teacher_features, Wk) + bk
        energy = jnp.einsum('bnd,bmd->bnm', query, key)
        attention = jax.nn.softmax(energy, axis=-1)
        x_m = jnp.einsum('bln,bmn->blm', teacher_logits, attention)
        return x_m

    def _L0_ffn_ref(hidden_states, gate_w, w_gate, w_up, w_down, sw_gate, sw_up, sw_down, shared_gate_w):
        import jax, jax.numpy as jnp
        import numpy as np
        B, S, H = (2, 256, 512)
        E, K = (8, 2)
        I = 352
        IS = 1408
        WSCALE = 0.02
        x = hidden_states
        logits = jnp.einsum('bsh,eh->bse', x, gate_w)
        probs = jax.nn.softmax(logits, axis=-1)
        top_w, top_i = jax.lax.top_k(probs, K)
        top_w = top_w / jnp.sum(top_w, axis=-1, keepdims=True)
        onehot = jax.nn.one_hot(top_i, E, dtype=x.dtype)
        combine = jnp.einsum('bsk,bske->bse', top_w, onehot)
        g = jnp.einsum('bsh,ehi->besi', x, w_gate)
        u = jnp.einsum('bsh,ehi->besi', x, w_up)
        h = jax.nn.silu(g) * u
        expert_out = jnp.einsum('besi,eih->besh', h, w_down)
        moe_out = jnp.einsum('besh,bse->bsh', expert_out, combine)
        sh = jax.nn.silu(x @ sw_gate) * (x @ sw_up)
        shared_out = sh @ sw_down
        shared_gate = jax.nn.sigmoid(x @ shared_gate_w)
        return moe_out + shared_out * shared_gate
    x = x + _L0_xattn_ref(_layernorm(x, axis=-1), ctx_1024, L0_xattn_Wq, L0_xattn_bq, L0_xattn_Wk, L0_xattn_bk)
    x = x + _L0_ffn_ref(_layernorm(x, axis=-1), L0_ffn_gate_w, L0_ffn_w_gate, L0_ffn_w_up, L0_ffn_w_down, L0_ffn_sw_gate, L0_ffn_sw_up, L0_ffn_sw_down, L0_ffn_shared_gate_w)
    return x

_drawn_inputs = setup_inputs


def setup_inputs(seed=0):
    import zlib

    import numpy as np

    out = dict(_drawn_inputs(seed))
    spreads = {'L0_xattn_bq': (0.0, 0.1), 'L0_xattn_bk': (0.0, 0.8)}
    factors = {'L0_ffn_gate_w': 2.869, 'L0_ffn_shared_gate_w': 7.884}
    for name, (base, spread) in spreads.items():
        noise = np.random.default_rng([zlib.crc32(name.encode()), seed]).standard_normal(out[name].shape)
        drawn = base * np.exp(spread * noise) if base else spread * noise
        out[name] = jnp.asarray(drawn.astype(out[name].dtype))
    for name, factor in factors.items():
        out[name] = (out[name] * factor).astype(out[name].dtype)
    return out
```

```python
from contextlib import ExitStack

import concourse.bass as bass
from concourse import mybir

ALU = mybir.AluOpType
ACT = mybir.ActivationFunctionType
AX = mybir.AxisListType
F32 = mybir.dt.float32
F16 = mybir.dt.float16
BF16 = mybir.dt.bfloat16

P = 128
HI, LO = 0, 1
PAIRS = ((HI, HI), (HI, LO), (LO, HI))
TOP_K = 2
ROUTE_STEPS = 11
GATE, UP, DOWN = 0, 1, 2


def build_xattn_moe(nc, x, ctx_in, w_q, b_q, w_k, b_k, gate_w, w_gate, w_up, w_down,
                    sw_gate, sw_up, sw_down, shared_gate_w, out, combine_dram):
    B, S, H = x.shape
    C = ctx_in.shape[2]
    E, _, I = w_gate.shape
    IS = sw_gate.shape[1]
    D = w_q.shape[0]
    RT = S // P
    KC = H // P
    CC = C // P
    EG = IS // I
    NG = E // EG + 1
    UT = IS // P
    NL = E + 1
    NC = NG * EG
    assert D == P and S == H and EG * I == IS and UT * P == IS and E % EG == 0
    EPS = 1e-5
    ATT_SCALE = 1024.0
    TURNS = CC + 3 * KC

    pieces = []
    for j in range(UT):
        cut, at = [], j * P
        while at < (j + 1) * P:
            e = at // I
            end = min((e + 1) * I, (j + 1) * P)
            cut.append((at - j * P, end - j * P, e))
            at = end
        pieces.append(cut)

    def legal(p0, p1):
        while p0 < p1:
            most = {0: 128, 32: 32, 64: 64, 96: 32}[p0]
            yield p0, min(p1, p0 + most)
            p0 = min(p1, p0 + most)

    with ExitStack() as stack:
        def sb(name, shape, dt):
            return stack.enter_context(nc.sbuf_tensor(name, shape, dt))

        def sem(name):
            return stack.enter_context(nc.semaphore(name))

        bank = [stack.enter_context(nc.psum_tensor(f"bank{i}", [P, 512], F32)) for i in range(8)]
        turn_ps = bank[0:2]
        q_ps, k_ps = bank[2], bank[3]
        energy_ps = bank[4:6]
        mix_ps = bank[6:8]
        gate_ps = [bank[0], bank[2]]
        up_ps = [bank[1], bank[3]]
        out_ps = bank[4:8]

        rows = sb("rows", [P, B * RT * H], F32)
        hT = sb("hT", [P, 2, KC, B * S], F16)
        weights = sb("weights", [P, UT, 2, 3, 512], BF16)
        staging = sb("staging", [P, 2, 3, 512], F32)
        ctx_sb = sb("ctx_sb", [P, RT, C], F32)
        normed = sb("normed", [P, RT, H], F32)
        xnT = sb("xnT", [P, 2, KC, S], F16)
        expo = sb("expo", [P, RT, S], F32)
        combineT = sb("combineT", [NC, B * S], F32)
        attn_space = sb("attn_space", [P, 2 * RT * S], F16)
        attnT = attn_space[:, :].rearrange("p (a t n) -> p a t n", a=2, t=RT)
        front = attn_space[:, :].bitcast(F32)
        ctxT = front[:, 0:CC * S].rearrange("p (c n) -> p c n", c=CC)
        qT = front[:, CC * S:CC * S + S]
        kT = front[:, CC * S + S:CC * S + 2 * S]
        combine_b = expo
        silu_sb, prod = normed[:, 0:2, :], normed[:, 2:4, :]
        hidden = xnT[:, :, :, :].rearrange("p a c n -> p (a c n)")[:, 0:6 * S].bitcast(BF16).rearrange(
            "p (r a n) -> p r a n", r=3, a=2)

        wqk = sb("wqk", [P, 2, C], F32)
        wqkT = sb("wqkT", [P, 2, CC, P], F32)
        bqk = sb("bqk", [P, 2], F32)
        gw_rows = sb("gw_rows", [NL, H], F32)
        gw_rest = sb("gw_rest", [P, 2, KC, NL], F32)
        gw3 = sb("gw3", [P, KC, 3, NL], BF16)
        ident = sb("ident", [P, P], F32)
        before = sb("before", [P, E, E], F32)
        minus_half = sb("minus_half", [P, RT], F32)
        stats = sb("stats", [P, 2, RT, 6], F32)
        mean_var = sb("mean_var", [P, 2, RT, 2], F32)
        var_eps = sb("var_eps", [P, 2, RT], F32)
        rstd = sb("rstd", [P, 2, RT], F32)
        neg_max = sb("neg_max", [P, RT], F32)
        exp_sum = sb("exp_sum", [P, RT], F32)
        sum_scaled = sb("sum_scaled", [P, RT], F32)
        inv_sum = sb("inv_sum", [P, RT], F32)
        logits = sb("logits", [P, RT, NL], F32)
        top = sb("top", [P, RT], F32)
        exp_in = sb("exp_in", [P, RT, NL], F32)
        exp_out = sb("exp_out", [P, RT, NL], F32)
        soft_sum = sb("soft_sum", [P, RT], F32)
        soft_inv = sb("soft_inv", [P, RT], F32)
        probs = sb("probs", [P, RT, E], F32)
        compared = wqk[:, :, :].rearrange("p a (t e j) -> p a t e j", t=RT, e=E)
        greater, equal = compared[:, 0], compared[:, 1]
        rank = sb("rank", [P, RT, E], F32)
        top_sum = sb("top_sum", [P, RT], F32)
        top_inv = sb("top_inv", [P, RT], F32)
        gate_den = sb("gate_den", [P, RT], F32)
        gate_val = sb("gate_val", [P, RT], F32)
        combine = sb("combine", [P, RT, NC], F32)
        carrier = sb("carrier", [P, 2], F32)

        x0_loaded, x_rest_loaded = sem("x0_loaded"), sem("x_rest_loaded")
        ctx_loaded = sem("ctx_loaded")
        wqk_loaded, gw_loaded = sem("wqk_loaded"), sem("gw_loaded")
        staged = [sem("staged0"), sem("staged1")]
        combine_stored = [sem(f"combine_stored{b}") for b in range(B)]
        combine_loaded, out_stored = sem("combine_loaded"), sem("out_stored")
        consts_zeroed, consts_ready = sem("consts_zeroed"), sem("consts_ready")
        wqk_turned, wqkT_ready = sem("wqk_turned"), sem("wqkT_ready")
        gw_turned, gw_step = sem("gw_turned"), sem("gw_step")
        stats_done, aggr_done = [sem("stats_done1"), sem("stats_done2")], [sem("aggr_done1"), sem("aggr_done2")]
        var_ready, rstd_ready = [sem("var_ready1"), sem("var_ready2")], [sem("rstd_ready1"), sem("rstd_ready2")]
        normed_ready = [sem("normed_ready1"), sem("normed_ready2")]
        turned = sem("turned")
        ctxT_ready, qk_done, qk_ready = sem("ctxT_ready"), sem("qk_done"), sem("qk_ready")
        xhi_ready, xlo_ready = sem("xhi_ready"), sem("xlo_ready")
        energy_done, max_ready, exp_done = sem("energy_done"), sem("max_ready"), sem("exp_done")
        sum_ready, inv_ready = sem("sum_ready"), sem("inv_ready")
        attn_ready = sem("attn_ready")
        ahi_ready, alo_ready = sem("ahi_ready"), sem("alo_ready")
        mix_done, added = sem("mix_done"), sem("added")
        hhi_ready, hlo_ready = sem("hhi_ready"), sem("hlo_ready")
        logits_done, logits_read = sem("logits_done"), sem("logits_read")
        r_step, exp_in_ready, r_exp = sem("r_step"), sem("exp_in_ready"), sem("r_exp")
        combine_ready, combine_turned, combineT_ready = sem("combine_ready"), sem("combine_turned"), sem("combineT_ready")
        high_split, split = sem("high_split"), sem("split")
        gate_done, up_done, down_done = sem("gate_done"), sem("up_done"), sem("down_done")
        silu_ready, prod_ready = sem("silu_ready"), sem("prod_ready")
        scaled, hid_hi, hid_lo = sem("scaled"), sem("hid_hi"), sem("hid_lo")
        block_summed = sem("block_summed")

        PRIME_ADDED, PRIME_HLO, PRIME_READ, PRIME = 2, 1, 1, 1

        def row_tile(b, i):
            return rows[:, bass.ds((b * RT + i) * H, H)]

        def first_turn(b):
            return 0 if isinstance(b, int) and b == 0 else b * TURNS - KC

        def h_turn(b, last):
            return b * TURNS + CC + 2 * KC if last else b * TURNS + 2 * CC + 3 * KC

        def attn_turn(b):
            return b * TURNS + CC + KC

        block = stack.enter_context(nc.Block())

        @block.sync
        def _(sp):
            rows_t = rows[:, :].rearrange("p (t h) -> p t h", h=H)

            def load_rows(b0, b1, x_sem):
                sp.dma_start(rows_t[:, b0 * RT:b1 * RT, :],
                             x[b0:b1].rearrange("b (t p) h -> p (b t) h", p=P)).then_inc(x_sem, 16)

            load_rows(0, 1, x0_loaded)
            sp.dma_start(wqk[:, 0, :], w_q).then_inc(wqk_loaded, 16)
            sp.dma_start(wqk[:, 1, :], w_k).then_inc(wqk_loaded, 16)
            sp.dma_start(bqk[:, 0:1], b_q.rearrange("(p a) -> p a", a=1)).then_inc(wqk_loaded, 16)
            sp.dma_start(bqk[:, 1:2], b_k.rearrange("(p a) -> p a", a=1)).then_inc(wqk_loaded, 16)
            sp.dma_start(gw_rows[0:E, :], gate_w).then_inc(gw_loaded, 16)
            sp.dma_start(gw_rows[E:NL, :], shared_gate_w.rearrange("h a -> a h")).then_inc(gw_loaded, 16)
            load_rows(1, B, x_rest_loaded)

            def load_unit_tile(g, j):
                n = g * UT + j
                if n >= 2:
                    sp.wait_ge(split, n - 1)
                slot = n % 2
                if g < NG - 1:
                    for kind, w in ((GATE, w_gate), (UP, w_up)):
                        dst = staging[:, slot, kind, :].rearrange("p (k u) -> p k u", k=KC)
                        for p0, p1, e in pieces[j]:
                            u0 = j * P + p0 - e * I
                            src = w[g * EG + e, :, u0:u0 + p1 - p0].rearrange("(k p) u -> p k u", p=P)
                            sp.dma_start(dst[:, :, p0:p1], src).then_inc(staged[slot], 16)
                    src = w_down.rearrange("e i h -> (e i) h")[(g * UT + j) * P:(g * UT + j + 1) * P, :]
                else:
                    for kind, w in ((GATE, sw_gate), (UP, sw_up)):
                        sp.dma_start(staging[:, slot, kind, :].rearrange("p (k u) -> p k u", k=KC),
                                     w[:, j * P:(j + 1) * P].rearrange("(k p) u -> p k u", p=P)
                                     ).then_inc(staged[slot], 16)
                    src = sw_down[j * P:(j + 1) * P, :]
                sp.dma_start(staging[:, slot, DOWN, :], src).then_inc(staged[slot], 16)

            def load_group(g):
                for j in range(UT):
                    load_unit_tile(g, j)

            load_group(0)
            for b in range(B):
                sp.wait_ge(combineT_ready, PRIME_READ + b + 1)
                sp.dma_start(combine_dram[:, b * S:(b + 1) * S],
                             combineT[:, b * S:(b + 1) * S]).then_inc(combine_stored[b], 16)
            for g in range(NG):
                for t in range(B):
                    n = g * B + t
                    if g == 0:
                        sp.wait_ge(combine_stored[t], 16)
                    if n == 0:
                        sp.wait_ge(alo_ready, RT * B)
                    else:
                        sp.wait_ge(scaled, UT * n)
                    src = combine_dram[g * EG:(g + 1) * EG, t * S:(t + 1) * S]
                    sp.dma_start(combine_b[:, :, :], src.partition_broadcast(P)).then_inc(combine_loaded, 16)
                if g < NG - 1:
                    load_group(g + 1)
            for t in range(B):
                sp.wait_ge(block_summed, PRIME + B * (NG - 1) + t + 1)
                sp.dma_start(out[t].rearrange("(t p) h -> p t h", p=P),
                             rows_t[:, t * RT:(t + 1) * RT, :]).then_inc(out_stored, 16)
            sp.wait_ge(out_stored, 16 * B)

        @block.gpsimd
        def _(pool):
            nc.gpsimd.memset(ident[:, :], 0.0).then_inc(consts_zeroed, 1)
            nc.gpsimd.memset(before[:, :, :], 1.0).then_inc(consts_zeroed, 1)
            nc.gpsimd.memset(minus_half[:, :], -0.5).then_inc(consts_ready, 1)
            pool.wait_ge(consts_zeroed, 2)
            nc.gpsimd.affine_select(out=ident[:, :], in_=ident[:, :], compare_op=ALU.not_equal, fill=1.0,
                                    base=0, pattern=[[-1, P]], channel_multiplier=1).then_inc(consts_ready, 1)
            nc.gpsimd.affine_select(out=before[:, :, :], in_=before[:, :, :], compare_op=ALU.is_gt, fill=0.0,
                                    base=0, pattern=[[1, E], [-1, E]], channel_multiplier=0).then_inc(consts_ready, 1)

            arrived = [0, 0]

            def split_unit_tile(g, j):
                slot = (g * UT + j) % 2
                n_dmas = 3 if g == NG - 1 else 1 + 2 * len(pieces[j])
                arrived[slot] += 16 * n_dmas
                pool.wait_ge(staged[slot], arrived[slot])
                if g > 0:
                    pool.wait_ge(down_done, PRIME + UT * (B * g - 1) + j + 1)
                nc.gpsimd.tensor_copy(weights[:, j, HI, :, :], staging[:, slot, :, :]).then_inc(high_split, 1)
                pool.wait_ge(high_split, g * UT + j + 1)
                nc.gpsimd.tensor_tensor(weights[:, j, LO, :, :], staging[:, slot, :, :], weights[:, j, HI, :, :],
                                        ALU.subtract).then_inc(split, 1)

            def inverse_deviation(which, b):
                pool.wait_ge(var_ready[which], b + 1)
                nc.gpsimd.tensor_tensor(rstd[:, which, :], var_eps[:, which, :], minus_half[:, :],
                                        ALU.pow).then_inc(rstd_ready[which], 1)

            pool.wait_ge(consts_ready, 3)
            inverse_deviation(0, 0)
            j = 0
            for b in range(B):
                if b + 1 < B:
                    inverse_deviation(0, b + 1)
                inverse_deviation(1, b)
                for _ in range(3):
                    if j < UT:
                        split_unit_tile(0, j)
                        j += 1
            for g in range(1, NG):
                for j in range(UT):
                    split_unit_tile(g, j)

        @block.scalar
        def _(act):
            def load_context(b):
                src = ctx_in[0] if isinstance(b, int) else ctx_in[bass.ds(b, 1)].rearrange("b s c -> (b s) c")
                act.dma_start(ctx_sb[:, :, :], src.rearrange("(t p) c -> p t c", p=P)).then_inc(ctx_loaded, 16)

            def context_turned(b):
                for c in range(CC):
                    act.wait_ge(turned, first_turn(b) + c + 1)
                    nc.scalar.copy(ctxT[:, c, :], turn_ps[c % 2][:, :]).then_inc(ctxT_ready, 1)

            def project(b):
                for i, ps in enumerate((q_ps, k_ps)):
                    act.wait_ge(qk_done, 2 * b + i + 1)
                    nc.scalar.activation((qT, kT)[i], ps[:, :], ACT.Identity,
                                         bias=bqk[:, i:i + 1]).then_inc(qk_ready, 1)

            def x_high(b):
                for c in range(KC):
                    act.wait_ge(turned, first_turn(b) + CC + c + 1)
                    nc.scalar.copy(xnT[:, HI, c, :], turn_ps[c % 2][:, :]).then_inc(xhi_ready, 1)

            def exponentials(b, first):
                for n in range(RT):
                    act.wait_ge(max_ready, RT * b + n + 1)
                    if not first:
                        act.wait_ge(alo_ready, RT * b)
                    nc.scalar.activation(expo[:, n, :], energy_ps[n % 2][:, :], ACT.Exp,
                                         bias=neg_max[:, n:n + 1],
                                         accum_out=exp_sum[:, n:n + 1]).then_inc(exp_done, 1)

            def h_high(b, last):
                for c in range(KC):
                    act.wait_ge(turned, h_turn(b, last) + c + 1)
                    nc.scalar.copy(hT[:, HI, c, bass.ds(b * S, S)], turn_ps[c % 2][:, :]).then_inc(hhi_ready, 1)

            def attn_high(b):
                for c in range(KC):
                    act.wait_ge(turned, attn_turn(b) + c + 1)
                    nc.scalar.copy(attnT[:, HI, c, :], turn_ps[c % 2][:, :]).then_inc(ahi_ready, 1)

            def router_exp(b):
                act.wait_ge(exp_in_ready, b + 1)
                nc.scalar.activation(exp_out[:, :, :], exp_in[:, :, :], ACT.Exp).then_inc(r_exp, 1)

            load_context(0)
            act.wait_ge(wqk_turned, 1)
            nc.scalar.copy(wqkT[:, :, :, :].rearrange("p a c d -> p (a c d)"),
                           q_ps[:, :]).then_inc(wqkT_ready, 1)
            act.wait_ge(wqk_loaded, 64)
            context_turned(0)
            project(0)
            x_high(0)
            exponentials(0, True)
            attn_high(0)
            with act.Fori(0, B - 1) as b:
                load_context(b + 1)
                context_turned(b + 1)
                project(b + 1)
                x_high(b + 1)
                exponentials(b + 1, False)
                h_high(b, False)
                attn_high(b + 1)
                router_exp(b)
            h_high(B - 1, True)
            router_exp(B - 1)

            with act.Fori(0, NG * B) as n:
                for j in range(UT):
                    act.wait_ge(gate_done, n * UT + j + 1)
                    act.wait_ge(prod_ready, n * UT + PRIME + max(0, j - 1))
                    nc.scalar.activation(silu_sb[:, j % 2, :], gate_ps[j % 2][:, :],
                                         ACT.Silu).then_inc(silu_ready, 1)
                    act.wait_ge(scaled, n * UT + j + 1)
                    act.wait_ge(down_done, n * UT + PRIME + max(0, j - 2))
                    nc.scalar.copy(hidden[:, j % 3, HI, :], prod[:, j % 2, :]).then_inc(hid_hi, 1)

        @block.vector
        def _(dve):
            def statistics(which, b):
                if which == 1:
                    dve.wait_ge(added, RT * b + PRIME_ADDED + RT)
                    nc.vector.memset(carrier[:, 1:2], 0.0)
                for i in range(RT):
                    op = nc.vector.bn_stats(stats[:, which, i, :], row_tile(b, i))
                op.then_inc(stats_done[which], 1)
                dve.wait_ge(stats_done[which], b + 1)
                nc.vector.memset(carrier[:, 0:1], 0.0)
                for i in range(RT):
                    op = nc.vector.bn_aggr(mean_var[:, which, i, :], stats[:, which, i, :])
                op.then_inc(aggr_done[which], 1)
                dve.wait_ge(aggr_done[which], b + 1)
                nc.vector.tensor_scalar(var_eps[:, which, :], mean_var[:, which, :, 1], EPS, None,
                                        ALU.add).then_inc(var_ready[which], 1)

            def normalize(which, b):
                dve.wait_ge(rstd_ready[which], b + 1)
                for i in range(RT):
                    op = nc.vector.tensor_scalar(normed[:, i, :], row_tile(b, i), mean_var[:, which, i, 0:1],
                                                 rstd[:, which, i:i + 1], ALU.subtract, ALU.mult)
                op.then_inc(normed_ready[which], 1)

            def x_low(b):
                for c in range(KC):
                    dve.wait_ge(xhi_ready, KC * b + c + 1)
                    nc.vector.tensor_tensor(xnT[:, LO, c, :], turn_ps[c % 2][:, :], xnT[:, HI, c, :],
                                            ALU.subtract).then_inc(xlo_ready, 1)

            def row_max(b):
                for n in range(RT):
                    dve.wait_ge(energy_done, RT * b + n + 1)
                    nc.vector.tensor_reduce(neg_max[:, n:n + 1], energy_ps[n % 2][:, :], AX.X, ALU.max,
                                            negate=True).then_inc(max_ready, 1)

            def inverse_sums(b):
                dve.wait_ge(exp_done, RT * b + RT)
                nc.vector.tensor_scalar(sum_scaled[:, :], exp_sum[:, :], 1.0 / ATT_SCALE, None,
                                        ALU.mult).then_inc(sum_ready, 1)
                dve.wait_ge(sum_ready, b + 1)
                nc.vector.reciprocal(inv_sum[:, :], sum_scaled[:, :]).then_inc(inv_ready, 1)

            def scale_attn(b):
                dve.wait_ge(inv_ready, b + 1)
                for n in range(RT):
                    op = nc.vector.tensor_scalar(expo[:, n, :], expo[:, n, :], inv_sum[:, n:n + 1], None, ALU.mult)
                op.then_inc(attn_ready, 1)

            def attn_low(b):
                for c in range(KC):
                    dve.wait_ge(ahi_ready, KC * b + c + 1)
                    nc.vector.tensor_tensor(attnT[:, LO, c, :], turn_ps[c % 2][:, :], attnT[:, HI, c, :],
                                            ALU.subtract).then_inc(alo_ready, 1)

            def add_mix(b):
                for i in range(RT):
                    dve.wait_ge(mix_done, RT * b + i + 1)
                    nc.vector.scalar_tensor_tensor(out=row_tile(b, i), in0=mix_ps[i % 2][:, :],
                                                   scalar=1.0 / ATT_SCALE, in1=row_tile(b, i),
                                                   op0=ALU.mult, op1=ALU.add).then_inc(added, 1)

            def h_low(b):
                for c in range(KC):
                    dve.wait_ge(hhi_ready, KC * b + c + 1)
                    cols = bass.ds(b * S, S)
                    nc.vector.tensor_tensor(hT[:, LO, c, cols], turn_ps[c % 2][:, :], hT[:, HI, c, cols],
                                            ALU.subtract).then_inc(hlo_ready, 1)

            def route(b):
                taken = [0]

                def step(op):
                    taken[0] += 1
                    op.then_inc(r_step, 1)
                    dve.wait_ge(r_step, ROUTE_STEPS * b + taken[0])

                def over_tile(a):
                    return a[:, :].unsqueeze(2).broadcast_to([P, RT, E])

                dve.wait_ge(logits_done, b + 1)
                parts = q_ps[:, 0:RT * 3 * NL].rearrange("p (t a e) -> p t e a", t=RT, a=3)
                nc.vector.tensor_reduce(logits[:, :, :], parts, AX.X, ALU.add).then_inc(logits_read, 1)
                dve.wait_ge(logits_read, PRIME_READ + b + 1)
                step(nc.vector.tensor_reduce(top[:, :], logits[:, :, 0:E], AX.X, ALU.max))
                nc.vector.tensor_scalar(exp_in[:, :, E], logits[:, :, E], -1.0, None, ALU.mult)
                nc.vector.tensor_tensor(exp_in[:, :, 0:E], logits[:, :, 0:E], over_tile(top),
                                        ALU.subtract).then_inc(exp_in_ready, 1)
                dve.wait_ge(r_exp, b + 1)
                nc.vector.tensor_scalar(gate_den[:, :], exp_out[:, :, E], 1.0, None, ALU.add)
                step(nc.vector.tensor_reduce(soft_sum[:, :], exp_out[:, :, 0:E], AX.X, ALU.add))
                nc.vector.reciprocal(gate_val[:, :], gate_den[:, :])
                step(nc.vector.reciprocal(soft_inv[:, :], soft_sum[:, :]))
                nc.vector.tensor_copy(combine[:, :, E:NC],
                                      gate_val[:, :].unsqueeze(2).broadcast_to([P, RT, NC - E]))
                step(nc.vector.tensor_tensor(probs[:, :, :], exp_out[:, :, 0:E], over_tile(soft_inv), ALU.mult))
                for i in range(RT):
                    p_other = probs[:, i, :].unsqueeze(1).broadcast_to([P, E, E])
                    p_own = probs[:, i, :].unsqueeze(2).broadcast_to([P, E, E])
                    nc.vector.tensor_tensor(greater[:, i, :, :], p_other, p_own, ALU.is_gt)
                    op = nc.vector.tensor_tensor(equal[:, i, :, :], p_other, p_own, ALU.is_equal)
                step(op)
                step(nc.vector.tensor_tensor(equal.rearrange("p t e j -> p t (e j)"),
                                             equal.rearrange("p t e j -> p t (e j)"),
                                             before[:, :, :].rearrange("p e j -> p (e j)").unsqueeze(1)
                                             .broadcast_to([P, RT, E * E]), ALU.mult))
                step(nc.vector.tensor_tensor(greater.rearrange("p t e j -> p (t e j)"),
                                             greater.rearrange("p t e j -> p (t e j)"),
                                             equal.rearrange("p t e j -> p (t e j)"), ALU.add))
                step(nc.vector.tensor_reduce(rank[:, :, :], greater, AX.X, ALU.add))
                step(nc.vector.scalar_tensor_tensor(out=rank[:, :, :], in0=rank[:, :, :], scalar=TOP_K - 0.5,
                                                    in1=probs[:, :, :], op0=ALU.is_lt, op1=ALU.mult))
                step(nc.vector.tensor_reduce(top_sum[:, :], rank[:, :, :], AX.X, ALU.add))
                step(nc.vector.reciprocal(top_inv[:, :], top_sum[:, :]))
                nc.vector.tensor_tensor(combine[:, :, 0:E], rank[:, :, :], over_tile(top_inv),
                                        ALU.mult).then_inc(combine_ready, 1)
                assert taken[0] == ROUTE_STEPS
                dve.wait_ge(combine_turned, b + 1)
                nc.vector.tensor_copy(combineT[:, bass.ds(b * S, S)], k_ps[0:NC, :]).then_inc(combineT_ready, 1)

            dve.sem_inc(added, PRIME_ADDED)
            dve.sem_inc(hlo_ready, PRIME_HLO)
            dve.sem_inc(logits_read, PRIME_READ)
            dve.sem_inc(combineT_ready, PRIME_READ)
            dve.sem_inc(silu_ready, PRIME)
            dve.sem_inc(prod_ready, PRIME)
            dve.sem_inc(down_done, PRIME)
            dve.sem_inc(block_summed, PRIME)

            dve.wait_ge(x0_loaded, 16)
            statistics(0, 0)
            normalize(0, 0)
            gw_ps = k_ps[:, 0:KC * NL].rearrange("p (k e) -> p k e", k=KC)
            dve.wait_ge(gw_turned, 1)
            nc.vector.tensor_copy(gw3[:, :, 0, :], gw_ps).then_inc(gw_step, 1)
            dve.wait_ge(gw_step, 1)
            nc.vector.tensor_tensor(gw_rest[:, 0, :, :], gw_ps, gw3[:, :, 0, :], ALU.subtract).then_inc(gw_step, 1)
            dve.wait_ge(gw_step, 2)
            nc.vector.tensor_copy(gw3[:, :, 1, :], gw_rest[:, 0, :, :]).then_inc(gw_step, 1)
            dve.wait_ge(gw_step, 3)
            nc.vector.tensor_tensor(gw_rest[:, 1, :, :], gw_rest[:, 0, :, :], gw3[:, :, 1, :],
                                    ALU.subtract).then_inc(gw_step, 1)
            dve.wait_ge(gw_step, 4)
            nc.vector.tensor_copy(gw3[:, :, 2, :], gw_rest[:, 1, :, :]).then_inc(gw_step, 1)
            x_low(0)
            row_max(0)
            inverse_sums(0)
            scale_attn(0)
            attn_low(0)
            dve.wait_ge(x_rest_loaded, 16)
            dve.wait_ge(consts_ready, 3)
            with dve.Fori(0, B - 1) as b:
                statistics(0, b + 1)
                normalize(0, b + 1)
                add_mix(b)
                statistics(1, b)
                x_low(b + 1)
                normalize(1, b)
                row_max(b + 1)
                h_low(b)
                inverse_sums(b + 1)
                scale_attn(b + 1)
                attn_low(b + 1)
                route(b)
            add_mix(B - 1)
            statistics(1, B - 1)
            normalize(1, B - 1)
            h_low(B - 1)
            route(B - 1)

            with dve.Fori(0, NG) as g:
                with dve.Fori(0, B) as t:
                    n = g * B + t
                    for j in range(UT):
                        dve.wait_ge(up_done, n * UT + j + 1)
                        dve.wait_ge(silu_ready, n * UT + PRIME + j + 1)
                        nc.vector.tensor_tensor(prod[:, j % 2, :], silu_sb[:, j % 2, :], up_ps[j % 2][:, :],
                                                ALU.mult).then_inc(prod_ready, 1)
                        dve.wait_ge(prod_ready, n * UT + PRIME + j + 1)
                        if j == 0:
                            dve.wait_ge(combine_loaded, n * 16 + 16)
                        for p0, p1, e in pieces[j]:
                            for a, z in legal(p0, p1):
                                op = nc.vector.tensor_tensor(prod[a:z, j % 2, :], prod[a:z, j % 2, :],
                                                             combine_b[a:z, e, :], ALU.mult)
                        op.then_inc(scaled, 1)
                        dve.wait_ge(hid_hi, n * UT + j + 1)
                        nc.vector.tensor_tensor(hidden[:, j % 3, LO, :], prod[:, j % 2, :], hidden[:, j % 3, HI, :],
                                                ALU.subtract).then_inc(hid_lo, 1)
                    dve.wait_ge(down_done, n * UT + PRIME + UT)
                    for i in range(RT):
                        op = nc.vector.tensor_tensor(row_tile(t, i), out_ps[i][:, :], row_tile(t, i), ALU.add)
                    op.then_inc(block_summed, 1)

        @block.tensor
        def _(pe):
            def turn_context(b):
                pe.wait_ge(ctx_loaded, 16 * b + 16)
                for c in range(CC):
                    for i in range(RT):
                        op = nc.tensor.transpose(turn_ps[c % 2][:, i * P:(i + 1) * P],
                                                 ctx_sb[:, i, c * P:(c + 1) * P], ident[:, :])
                    op.then_inc(turned, 1)

            def project(b):
                for i, ps in enumerate((q_ps, k_ps)):
                    for c in range(CC):
                        if i == 0:
                            pe.wait_ge(ctxT_ready, CC * b + c + 1)
                        op = nc.tensor.matmul(ps[:, :], wqkT[:, i, c, :], ctxT[:, c, :],
                                              start=(c == 0), stop=(c == CC - 1))
                    op.then_inc(qk_done, 1)

            def turn_x(b):
                pe.wait_ge(normed_ready[0], b + 1)
                for c in range(KC):
                    if c >= 2:
                        pe.wait_ge(xlo_ready, KC * b + c - 1)
                    for i in range(RT):
                        op = nc.tensor.transpose(turn_ps[c % 2][:, i * P:(i + 1) * P],
                                                 normed[:, i, c * P:(c + 1) * P], ident[:, :])
                    op.then_inc(turned, 1)

            def energies(b, first):
                pe.wait_ge(qk_ready, 2 * b + 2)
                for n in range(RT):
                    if not (first and n < 2):
                        pe.wait_ge(exp_done, RT * b + n - 1)
                    nc.tensor.matmul(energy_ps[n % 2][:, :], qT[:, n * P:(n + 1) * P], kT,
                                     start=True, stop=True).then_inc(energy_done, 1)

            def turn_attn(b, first):
                pe.wait_ge(attn_ready, b + 1)
                for c in range(KC):
                    if c >= 2:
                        pe.wait_ge(alo_ready, KC * b + c - 1)
                    elif first:
                        pe.wait_ge(xlo_ready, KC)
                    for m in range(RT):
                        op = nc.tensor.transpose(turn_ps[c % 2][:, m * P:(m + 1) * P],
                                                 expo[:, m, c * P:(c + 1) * P], ident[:, :])
                    op.then_inc(turned, 1)

            def mix(b):
                pe.wait_ge(xlo_ready, KC * b + KC)
                pe.wait_ge(alo_ready, RT * b + RT)
                for i in range(RT):
                    pe.wait_ge(added, RT * b + PRIME_ADDED + i - 1)
                    for c in range(KC):
                        for s, (xp, ap) in enumerate(PAIRS):
                            op = nc.tensor.matmul(mix_ps[i % 2][:, :], xnT[:, xp, c, i * P:(i + 1) * P],
                                                  attnT[:, ap, c, :], start=(c == 0 and s == 0),
                                                  stop=(c == KC - 1 and s == len(PAIRS) - 1))
                    op.then_inc(mix_done, 1)

            def turn_h(b, last):
                pe.wait_ge(normed_ready[1], b + 1)
                for c in range(KC):
                    if c >= 2:
                        pe.wait_ge(hlo_ready, KC * b + PRIME_HLO + c - 1)
                    elif not last:
                        pe.wait_ge(xlo_ready, KC * b + KC + c + 3)
                    for i in range(RT):
                        op = nc.tensor.transpose(turn_ps[c % 2][:, i * P:(i + 1) * P],
                                                 normed[:, i, c * P:(c + 1) * P], ident[:, :])
                    op.then_inc(turned, 1)

            def router_logits(b):
                pe.wait_ge(hlo_ready, KC * b + PRIME_HLO + KC)
                pe.wait_ge(logits_read, b + PRIME_READ)
                for i in range(RT):
                    for c in range(KC):
                        for part in (HI, LO):
                            op = nc.tensor.matmul(q_ps[:, i * 3 * NL:(i + 1) * 3 * NL],
                                                  hT[:, part, c, bass.ds(b * S + i * P, P)],
                                                  gw3[:, c, :, :].rearrange("p a e -> p (a e)"),
                                                  start=(c == 0 and part == HI), stop=(c == KC - 1 and part == LO))
                op.then_inc(logits_done, 1)

            def turn_combine(b):
                pe.wait_ge(combine_ready, b + 1)
                for i in range(RT):
                    op = nc.tensor.transpose(k_ps[0:NC, i * P:(i + 1) * P], combine[:, i, :], ident[:, :])
                op.then_inc(combine_turned, 1)

            pe.wait_ge(consts_ready, 3)
            pe.wait_ge(wqk_loaded, 64)
            for i in range(2):
                for c in range(CC):
                    op = nc.tensor.transpose(q_ps[:, (i * CC + c) * P:(i * CC + c + 1) * P],
                                             wqk[:, i, c * P:(c + 1) * P], ident[:, :])
            op.then_inc(wqk_turned, 1)
            pe.wait_ge(gw_loaded, 32)
            for c in range(KC):
                op = nc.tensor.transpose(k_ps[:, c * NL:(c + 1) * NL], gw_rows[:, c * P:(c + 1) * P],
                                         ident[0:NL, 0:NL])
            op.then_inc(gw_turned, 1)
            turn_context(0)
            pe.wait_ge(wqkT_ready, 1)
            pe.wait_ge(gw_step, 5)
            project(0)
            turn_x(0)
            energies(0, True)
            turn_attn(0, True)
            with pe.Fori(0, B - 1) as b:
                mix(b)
                turn_context(b + 1)
                pe.wait_ge(logits_read, b + PRIME_READ)
                pe.wait_ge(combineT_ready, b + PRIME_READ)
                project(b + 1)
                turn_x(b + 1)
                energies(b + 1, False)
                turn_h(b, False)
                router_logits(b)
                turn_attn(b + 1, False)
                turn_combine(b)
            mix(B - 1)
            turn_h(B - 1, True)
            router_logits(B - 1)
            turn_combine(B - 1)
            pe.wait_ge(combineT_ready, B + PRIME_READ)

            with pe.Fori(0, NG) as g:
                with pe.Fori(0, B) as t:
                    n = g * B + t

                    def gate_and_up(j):
                        pe.wait_ge(split, g * UT + j + 1)
                        for kind, banks, done, free in ((GATE, gate_ps, gate_done, silu_ready),
                                                        (UP, up_ps, up_done, prod_ready)):
                            pe.wait_ge(free, n * UT + PRIME + max(0, j - 1))
                            for c in range(KC):
                                for s, (wp, hp) in enumerate(PAIRS):
                                    op = nc.tensor.matmul(banks[j % 2][:, :],
                                                          weights[:, j, wp, kind, c * P:(c + 1) * P],
                                                          hT[:, hp, c, bass.ds(t * S, S)],
                                                          start=(c == 0 and s == 0),
                                                          stop=(c == KC - 1 and s == len(PAIRS) - 1))
                            op.then_inc(done, 1)

                    def down(j):
                        pe.wait_ge(hid_lo, n * UT + j + 1)
                        if j == 0:
                            pe.wait_ge(block_summed, n + PRIME)
                        for i in range(RT):
                            for s, (hp, wp) in enumerate(PAIRS):
                                op = nc.tensor.matmul(out_ps[i][:, :], hidden[:, j % 3, hp, i * P:(i + 1) * P],
                                                      weights[:, j, wp, DOWN, :], start=(j == 0 and s == 0),
                                                      stop=(j == UT - 1 and s == len(PAIRS) - 1))
                        op.then_inc(down_done, 1)

                    for j in range(UT + 2):
                        if j < UT:
                            gate_and_up(j)
                        if j >= 2:
                            down(j - 2)


_INS = ["x", "ctx_1024", "L0_xattn_Wq", "L0_xattn_bq", "L0_xattn_Wk", "L0_xattn_bk", "L0_ffn_gate_w",
        "L0_ffn_w_gate", "L0_ffn_w_up", "L0_ffn_w_down", "L0_ffn_sw_gate", "L0_ffn_sw_up", "L0_ffn_sw_down",
        "L0_ffn_shared_gate_w"]


def kernel(**inputs):
    import numpy as np
    import concourse.bacc as bacc
    from concourse.bass_utils import run_bass_kernel_spmd

    nc = bacc.Bacc("TRN2", target_bir_lowering=False, num_devices=1)
    arrays, args = {}, []
    for name in _INS:
        a = np.ascontiguousarray(inputs[name])
        arrays[name] = a
        args.append(nc.dram_tensor(name, a.shape, mybir.dt.from_np(a.dtype), kind="ExternalInput").ap())
    shape = inputs["x"].shape
    out = nc.dram_tensor("out", shape, F32, kind="ExternalOutput").ap()
    combine_dram = nc.dram_tensor("combine_dram", (12, shape[0] * shape[1]), F32, kind="Internal").ap()
    build_xattn_moe(nc, *args, out, combine_dram)
    r = run_bass_kernel_spmd(nc, [arrays], core_ids=[0])
    return r.results[0]["out"]
```

```python
from contextlib import ExitStack

import concourse.bass as bass
from concourse import mybir

ALU = mybir.AluOpType
ACT = mybir.ActivationFunctionType
AX = mybir.AxisListType
F32 = mybir.dt.float32
F16 = mybir.dt.float16
BF16 = mybir.dt.bfloat16

P = 128
HI, LO = 0, 1
PAIRS = ((HI, HI), (HI, LO), (LO, HI))
TOP_K = 2
EARLY = 5
AT_POINT = {
    (0, "start"): [("load", 0), ("stats1", 0)],
    (0, "up"): [("ctx", 0)],
    (1, "gate"): [("ctx", 1)],
    (1, "up"): [("qk", 0)],
    (1, "down"): [("norm1", 0)],
    (2, "gate"): [("qk", 1)],
    (2, "up"): [("energy", 0)],
    (2, "down"): [("energy", 1)],
    (3, "gate"): [("energy", 2)],
    (3, "up"): [("energy", 3)],
    (3, "down"): [("x", 0), ("scale", 0)],
    (4, "gate"): [("x", 1)],
    (4, "up"): [("x", 2)],
    (4, "down"): [("x", 3)],
    (5, "gate"): [("attn", 0)],
    (5, "up"): [("attn", 1)],
    (5, "down"): [("attn", 2)],
    (6, "gate"): [("attn", 3)],
    (6, "up"): [("mix", 0)],
    (6, "down"): [("mix", 1)],
    (7, "gate"): [("mix", 2)],
    (7, "up"): [("mix", 3)],
    (7, "down"): [("stats2", 0)],
    (8, "start"): [("norm2", 0)],
    (8, "up"): [("h", 0)],
    (8, "down"): [("h", 1)],
    (9, "gate"): [("h", 2)],
    (9, "up"): [("h", 3)],
    (9, "down"): [("logits", 0)],
    (10, "gate"): [("route", 0)],
    (10, "down"): [("combine", 0)],
}
ROUTE_STEPS = 11
GATE, UP, DOWN = 0, 1, 2


def build_xattn_moe(nc, x, ctx_in, w_q, b_q, w_k, b_k, gate_w, w_gate, w_up, w_down,
                    sw_gate, sw_up, sw_down, shared_gate_w, out, combine_dram):
    B, S, H = x.shape
    C = ctx_in.shape[2]
    E, _, I = w_gate.shape
    IS = sw_gate.shape[1]
    D = w_q.shape[0]
    RT = S // P
    KC = H // P
    CC = C // P
    EG = IS // I
    NG = E // EG + 1
    UT = IS // P
    NL = E + 1
    NC = NG * EG
    assert D == P and S == H and EG * I == IS and UT * P == IS and E % EG == 0
    EPS = 1e-5
    ATT_SCALE = 1024.0
    TURNS = CC + 3 * KC

    pieces = []
    for j in range(UT):
        cut, at = [], j * P
        while at < (j + 1) * P:
            e = at // I
            end = min((e + 1) * I, (j + 1) * P)
            cut.append((at - j * P, end - j * P, e))
            at = end
        pieces.append(cut)

    def legal(p0, p1):
        while p0 < p1:
            most = {0: 128, 32: 32, 64: 64, 96: 32}[p0]
            yield p0, min(p1, p0 + most)
            p0 = min(p1, p0 + most)

    with ExitStack() as stack:
        def sb(name, shape, dt):
            return stack.enter_context(nc.sbuf_tensor(name, shape, dt))

        def sem(name):
            return stack.enter_context(nc.semaphore(name))

        bank = [stack.enter_context(nc.psum_tensor(f"bank{i}", [P, 512], F32)) for i in range(8)]
        gate_ps, up_ps, out_ps = bank[2], bank[3], bank[4:8]

        def att_bank(b, stage, i):
            if isinstance(b, int) and b == 0:
                first = {"ctx": 0, "qk": 2, "energy": 4, "x": 0, "attn": 4, "mix": 0, "h": 4, "logits": 0, "combine": 1}
                return bank[first[stage] + i]
            return bank[1] if stage == "combine" else bank[i % 2]

        rows = sb("rows", [P, B * RT * H], F32)
        hT = sb("hT", [P, 2, KC, B * S], F16)
        weights = sb("weights", [P, UT, 2, 3, 512], BF16)
        staging = sb("staging", [P, 2, 3, 512], F32)
        ctx_sb = sb("ctx_sb", [P, RT, C], F32)
        normed = sb("normed", [P, RT, H], F32)
        xnT = sb("xnT", [P, 2, KC, S], F16)
        expo = sb("expo", [P, RT, S], F32)
        combineT = sb("combineT", [NC, S], F32)
        attn_space = sb("attn_space", [P, 2 * RT * S], F16)
        attnT = attn_space[:, :].rearrange("p (a t n) -> p a t n", a=2, t=RT)
        front = attn_space[:, :].bitcast(F32)
        ctxT = front[:, 0:CC * S].rearrange("p (c n) -> p c n", c=CC)
        qT = front[:, CC * S:CC * S + S]
        kT = front[:, CC * S + S:CC * S + 2 * S]
        combine_b = sb("combine_b", [P, EG, S], F32)
        silu_sb = sb("silu_sb", [P, S], F32)
        prod = sb("prod", [P, S], F32)
        hidden = sb("hidden", [P, 3, 2, S], BF16)

        wqk = sb("wqk", [P, 2, C], F32)
        wqkT = sb("wqkT", [P, 2, CC, P], F32)
        bqk = sb("bqk", [P, 2], F32)
        gw_rows = combineT[0:NL, :]
        gw_rest = sb("gw_rest", [P, 2, KC, NL], F32)
        gw3 = sb("gw3", [P, KC, 3, NL], BF16)
        ident = sb("ident", [P, P], F32)
        before = sb("before", [P, E, E], F32)
        minus_half = sb("minus_half", [P, RT], F32)
        stats = sb("stats", [P, 2, RT, 6], F32)
        mean_var = sb("mean_var", [P, 2, RT, 2], F32)
        var_eps = sb("var_eps", [P, 2, RT], F32)
        rstd = sb("rstd", [P, 2, RT], F32)
        neg_max = sb("neg_max", [P, RT], F32)
        exp_sum = sb("exp_sum", [P, RT], F32)
        sum_scaled = sb("sum_scaled", [P, RT], F32)
        inv_sum = sb("inv_sum", [P, RT], F32)
        logits = sb("logits", [P, RT, NL], F32)
        top = sb("top", [P, RT], F32)
        exp_in = sb("exp_in", [P, RT, NL], F32)
        exp_out = sb("exp_out", [P, RT, NL], F32)
        soft_sum = sb("soft_sum", [P, RT], F32)
        soft_inv = sb("soft_inv", [P, RT], F32)
        probs = sb("probs", [P, RT, E], F32)
        compared = wqk[:, :, :].rearrange("p a (t e j) -> p a t e j", t=RT, e=E)
        greater, equal = compared[:, 0], compared[:, 1]
        rank = sb("rank", [P, RT, E], F32)
        top_sum = sb("top_sum", [P, RT], F32)
        top_inv = sb("top_inv", [P, RT], F32)
        gate_den = sb("gate_den", [P, RT], F32)
        gate_val = sb("gate_val", [P, RT], F32)
        combine = sb("combine", [P, RT, NC], F32)
        carrier = sb("carrier", [P, 2], F32)

        x0_loaded, x_rest_loaded = sem("x0_loaded"), sem("x_rest_loaded")
        ctx_loaded = sem("ctx_loaded")
        wqk_loaded, gw_loaded = sem("wqk_loaded"), sem("gw_loaded")
        staged = [sem("staged0"), sem("staged1")]
        combine_stored = sem("combine_stored")
        combine_loaded, out_stored = sem("combine_loaded"), sem("out_stored")
        consts_zeroed, consts_ready = sem("consts_zeroed"), sem("consts_ready")
        wqk_turned, wqkT_ready = sem("wqk_turned"), sem("wqkT_ready")
        gw_turned, gw_step = sem("gw_turned"), sem("gw_step")
        stats_done, aggr_done = [sem("stats_done1"), sem("stats_done2")], [sem("aggr_done1"), sem("aggr_done2")]
        var_ready, rstd_ready = [sem("var_ready1"), sem("var_ready2")], [sem("rstd_ready1"), sem("rstd_ready2")]
        normed_ready = [sem("normed_ready1"), sem("normed_ready2")]
        turned = sem("turned")
        ctxT_ready, qk_done, qk_ready = sem("ctxT_ready"), sem("qk_done"), sem("qk_ready")
        xhi_ready, xlo_ready = sem("xhi_ready"), sem("xlo_ready")
        energy_done, max_ready, exp_done = sem("energy_done"), sem("max_ready"), sem("exp_done")
        sum_ready, inv_ready = sem("sum_ready"), sem("inv_ready")
        attn_ready = sem("attn_ready")
        ahi_ready, alo_ready = sem("ahi_ready"), sem("alo_ready")
        mix_done, added = sem("mix_done"), sem("added")
        hhi_ready, hlo_ready = sem("hhi_ready"), sem("hlo_ready")
        logits_done, logits_read = sem("logits_done"), sem("logits_read")
        r_step, exp_in_ready, r_exp = sem("r_step"), sem("exp_in_ready"), sem("r_exp")
        combine_ready, combine_turned, combineT_ready = sem("combine_ready"), sem("combine_turned"), sem("combineT_ready")
        high_split, split = sem("high_split"), sem("split")
        gate_done, up_done, down_done = sem("gate_done"), sem("up_done"), sem("down_done")
        silu_ready, prod_ready = sem("silu_ready"), sem("prod_ready")
        scaled, hid_hi, hid_lo = sem("scaled"), sem("hid_hi"), sem("hid_lo")
        block_summed = sem("block_summed")

        PRIME = 1

        def row_tile(b, i):
            return rows[:, bass.ds((b * RT + i) * H, H)]

        def turn_count(b, stage):
            return b * TURNS + {"ctx": 0, "x": CC, "attn": CC + KC, "h": CC + 2 * KC}[stage]

        block = stack.enter_context(nc.Block())

        @block.sync
        def _(sp):
            rows_t = rows[:, :].rearrange("p (t h) -> p t h", h=H)

            def load_rows(b0, b1, x_sem):
                sp.dma_start(rows_t[:, b0 * RT:b1 * RT, :],
                             x[b0:b1].rearrange("b (t p) h -> p (b t) h", p=P)).then_inc(x_sem, 16)

            load_rows(0, 1, x0_loaded)
            sp.dma_start(wqk[:, 0, :], w_q).then_inc(wqk_loaded, 16)
            sp.dma_start(wqk[:, 1, :], w_k).then_inc(wqk_loaded, 16)
            sp.dma_start(bqk[:, 0:1], b_q.rearrange("(p a) -> p a", a=1)).then_inc(wqk_loaded, 16)
            sp.dma_start(bqk[:, 1:2], b_k.rearrange("(p a) -> p a", a=1)).then_inc(wqk_loaded, 16)
            sp.dma_start(gw_rows[0:E, :], gate_w).then_inc(gw_loaded, 16)
            sp.dma_start(gw_rows[E:NL, :], shared_gate_w.rearrange("h a -> a h")).then_inc(gw_loaded, 16)
            load_rows(1, B, x_rest_loaded)

            def load_unit_tile(g, j):
                n = g * UT + j
                if n >= 2:
                    sp.wait_ge(split, n - 1)
                slot = n % 2
                if g < NG - 1:
                    for kind, w in ((GATE, w_gate), (UP, w_up)):
                        dst = staging[:, slot, kind, :].rearrange("p (k u) -> p k u", k=KC)
                        for p0, p1, e in pieces[j]:
                            u0 = j * P + p0 - e * I
                            src = w[g * EG + e, :, u0:u0 + p1 - p0].rearrange("(k p) u -> p k u", p=P)
                            sp.dma_start(dst[:, :, p0:p1], src).then_inc(staged[slot], 16)
                    src = w_down.rearrange("e i h -> (e i) h")[(g * UT + j) * P:(g * UT + j + 1) * P, :]
                else:
                    for kind, w in ((GATE, sw_gate), (UP, sw_up)):
                        sp.dma_start(staging[:, slot, kind, :].rearrange("p (k u) -> p k u", k=KC),
                                     w[:, j * P:(j + 1) * P].rearrange("(k p) u -> p k u", p=P)
                                     ).then_inc(staged[slot], 16)
                    src = sw_down[j * P:(j + 1) * P, :]
                sp.dma_start(staging[:, slot, DOWN, :], src).then_inc(staged[slot], 16)

            def load_group(g):
                for j in range(UT):
                    load_unit_tile(g, j)

            def share_combine(b):
                sp.wait_ge(combineT_ready, b + 1)
                sp.dma_start(combine_dram[:, b * S:(b + 1) * S], combineT[:, :]).then_inc(combine_stored, 16)
                sp.wait_ge(combine_stored, 16 * (b + 1))

            def load_combine(g, t):
                n = g * B + t
                if n:
                    sp.wait_ge(scaled, UT * n)
                src = combine_dram[g * EG:(g + 1) * EG, t * S:(t + 1) * S]
                sp.dma_start(combine_b[:, :, :], src.partition_broadcast(P)).then_inc(combine_loaded, 16)

            for j in range(EARLY):
                load_unit_tile(0, j)
            share_combine(0)
            load_combine(0, 0)
            for j in range(EARLY, UT):
                load_unit_tile(0, j)
            for t in range(1, B):
                share_combine(t)
                load_combine(0, t)
            for g in range(1, NG):
                load_group(g)
                for t in range(B):
                    load_combine(g, t)
            for t in range(B):
                sp.wait_ge(block_summed, PRIME + B * (NG - 1) + t + 1)
                sp.dma_start(out[t].rearrange("(t p) h -> p t h", p=P),
                             rows_t[:, t * RT:(t + 1) * RT, :]).then_inc(out_stored, 16)
            sp.wait_ge(out_stored, 16 * B)

        @block.gpsimd
        def _(pool):
            nc.gpsimd.memset(ident[:, :], 0.0).then_inc(consts_zeroed, 1)
            nc.gpsimd.memset(before[:, :, :], 1.0).then_inc(consts_zeroed, 1)
            nc.gpsimd.memset(minus_half[:, :], -0.5).then_inc(consts_ready, 1)
            pool.wait_ge(consts_zeroed, 2)
            nc.gpsimd.affine_select(out=ident[:, :], in_=ident[:, :], compare_op=ALU.not_equal, fill=1.0,
                                    base=0, pattern=[[-1, P]], channel_multiplier=1).then_inc(consts_ready, 1)
            nc.gpsimd.affine_select(out=before[:, :, :], in_=before[:, :, :], compare_op=ALU.is_gt, fill=0.0,
                                    base=0, pattern=[[1, E], [-1, E]], channel_multiplier=0).then_inc(consts_ready, 1)

            arrived = [0, 0]

            def split_unit_tile(g, j):
                slot = (g * UT + j) % 2
                n_dmas = 3 if g == NG - 1 else 1 + 2 * len(pieces[j])
                arrived[slot] += 16 * n_dmas
                pool.wait_ge(staged[slot], arrived[slot])
                if g > 0:
                    pool.wait_ge(down_done, PRIME + UT * (B * g - 1) + j + 1)
                nc.gpsimd.tensor_copy(weights[:, j, HI, :, :], staging[:, slot, :, :]).then_inc(high_split, 1)
                pool.wait_ge(high_split, g * UT + j + 1)
                nc.gpsimd.tensor_tensor(weights[:, j, LO, :, :], staging[:, slot, :, :], weights[:, j, HI, :, :],
                                        ALU.subtract).then_inc(split, 1)

            def inverse_deviation(which, b):
                pool.wait_ge(var_ready[which], b + 1)
                nc.gpsimd.tensor_tensor(rstd[:, which, :], var_eps[:, which, :], minus_half[:, :],
                                        ALU.pow).then_inc(rstd_ready[which], 1)

            pool.wait_ge(consts_ready, 3)
            inverse_deviation(0, 0)
            for j in range(0, 2):
                split_unit_tile(0, j)
            inverse_deviation(1, 0)
            for j in range(2, EARLY):
                split_unit_tile(0, j)
            inverse_deviation(0, 1)
            for j in range(EARLY, UT):
                split_unit_tile(0, j)
            inverse_deviation(1, 1)
            for b in range(2, B):
                inverse_deviation(0, b)
                inverse_deviation(1, b)
            for g in range(1, NG):
                for j in range(UT):
                    split_unit_tile(g, j)

        @block.scalar
        def _(act):
            def load_context(b):
                src = ctx_in[0] if isinstance(b, int) else ctx_in[bass.ds(b, 1)].rearrange("b s c -> (b s) c")
                act.dma_start(ctx_sb[:, :, :], src.rearrange("(t p) c -> p t c", p=P)).then_inc(ctx_loaded, 16)

            def context_turned(b, c):
                act.wait_ge(turned, turn_count(b, "ctx") + c + 1)
                nc.scalar.copy(ctxT[:, c, :], att_bank(b, "ctx", c)[:, :]).then_inc(ctxT_ready, 1)

            def project(b, i):
                act.wait_ge(qk_done, 2 * b + i + 1)
                nc.scalar.activation((qT, kT)[i], att_bank(b, "qk", i)[:, :], ACT.Identity,
                                     bias=bqk[:, i:i + 1]).then_inc(qk_ready, 1)

            def exponential(b, n):
                act.wait_ge(max_ready, RT * b + n + 1)
                nc.scalar.activation(expo[:, n, :], att_bank(b, "energy", n)[:, :], ACT.Exp,
                                     bias=neg_max[:, n:n + 1],
                                     accum_out=exp_sum[:, n:n + 1]).then_inc(exp_done, 1)

            def x_high(b, c):
                act.wait_ge(turned, turn_count(b, "x") + c + 1)
                nc.scalar.copy(xnT[:, HI, c, :], att_bank(b, "x", c)[:, :]).then_inc(xhi_ready, 1)

            def attn_high(b, c):
                act.wait_ge(turned, turn_count(b, "attn") + c + 1)
                nc.scalar.copy(attnT[:, HI, c, :], att_bank(b, "attn", c)[:, :]).then_inc(ahi_ready, 1)

            def h_high(b, c):
                act.wait_ge(turned, turn_count(b, "h") + c + 1)
                nc.scalar.copy(hT[:, HI, c, bass.ds(b * S, S)], att_bank(b, "h", c)[:, :]).then_inc(hhi_ready, 1)

            def router_exp(b):
                act.wait_ge(exp_in_ready, b + 1)
                nc.scalar.activation(exp_out[:, :, :], exp_in[:, :, :], ACT.Exp).then_inc(r_exp, 1)

            load_context(0)
            act.wait_ge(wqk_turned, 1)
            nc.scalar.copy(wqkT[:, :, :, :].rearrange("p a c d -> p (a c d)"),
                           bank[2][:, :]).then_inc(wqkT_ready, 1)
            act.wait_ge(wqk_loaded, 64)
            for c in range(CC):
                context_turned(0, c)
            for i in range(2):
                project(0, i)
            for n in range(RT):
                exponential(0, n)
            for c in range(KC):
                x_high(0, c)
            for c in range(KC):
                attn_high(0, c)
            for c in range(KC):
                h_high(0, c)
            router_exp(0)

            def attention(j, point, b):
                for stage, i in AT_POINT.get((j, point), ()):
                    if stage == "load":
                        load_context(b)
                    elif stage == "ctx":
                        context_turned(b, i)
                    elif stage == "qk":
                        project(b, i)
                    elif stage == "energy":
                        exponential(b, i)
                    elif stage == "x":
                        x_high(b, i)
                    elif stage == "attn":
                        attn_high(b, i)
                    elif stage == "h":
                        h_high(b, i)
                    elif stage == "logits":
                        router_exp(b)

            def ffn_block(n, b=None):
                def beside(j, point):
                    if b is not None:
                        attention(j, point, b)

                for j in range(UT):
                    beside(j, "start")
                    act.wait_ge(gate_done, n * UT + j + 1)
                    act.wait_ge(prod_ready, n * UT + PRIME + j)
                    nc.scalar.activation(silu_sb[:, :], gate_ps[:, :], ACT.Silu).then_inc(silu_ready, 1)
                    beside(j, "gate")
                    beside(j, "up")
                    act.wait_ge(scaled, n * UT + j + 1)
                    act.wait_ge(down_done, n * UT + PRIME + max(0, j - 2))
                    nc.scalar.copy(hidden[:, j % 3, HI, :], prod[:, :]).then_inc(hid_hi, 1)
                    beside(j, "down")

            with act.Fori(0, B - 1) as t:
                ffn_block(t, t + 1)
            with act.Fori(B - 1, NG * B) as n:
                ffn_block(n)

        @block.vector
        def _(dve):
            def statistics(which, b):
                if which == 1:
                    dve.wait_ge(added, RT * b + RT)
                    nc.vector.memset(carrier[:, 1:2], 0.0)
                for i in range(RT):
                    op = nc.vector.bn_stats(stats[:, which, i, :], row_tile(b, i))
                op.then_inc(stats_done[which], 1)
                dve.wait_ge(stats_done[which], b + 1)
                nc.vector.memset(carrier[:, 0:1], 0.0)
                for i in range(RT):
                    op = nc.vector.bn_aggr(mean_var[:, which, i, :], stats[:, which, i, :])
                op.then_inc(aggr_done[which], 1)
                dve.wait_ge(aggr_done[which], b + 1)
                nc.vector.tensor_scalar(var_eps[:, which, :], mean_var[:, which, :, 1], EPS, None,
                                        ALU.add).then_inc(var_ready[which], 1)

            def normalize(which, b):
                dve.wait_ge(rstd_ready[which], b + 1)
                for i in range(RT):
                    op = nc.vector.tensor_scalar(normed[:, i, :], row_tile(b, i), mean_var[:, which, i, 0:1],
                                                 rstd[:, which, i:i + 1], ALU.subtract, ALU.mult)
                op.then_inc(normed_ready[which], 1)

            def x_low(b, c):
                dve.wait_ge(xhi_ready, KC * b + c + 1)
                nc.vector.tensor_tensor(xnT[:, LO, c, :], att_bank(b, "x", c)[:, :], xnT[:, HI, c, :],
                                        ALU.subtract).then_inc(xlo_ready, 1)

            def row_max(b, n):
                dve.wait_ge(energy_done, RT * b + n + 1)
                nc.vector.tensor_reduce(neg_max[:, n:n + 1], att_bank(b, "energy", n)[:, :], AX.X, ALU.max,
                                        negate=True).then_inc(max_ready, 1)

            def scale_attn(b):
                dve.wait_ge(exp_done, RT * b + RT)
                nc.vector.tensor_scalar(sum_scaled[:, :], exp_sum[:, :], 1.0 / ATT_SCALE, None,
                                        ALU.mult).then_inc(sum_ready, 1)
                dve.wait_ge(sum_ready, b + 1)
                nc.vector.reciprocal(inv_sum[:, :], sum_scaled[:, :]).then_inc(inv_ready, 1)
                dve.wait_ge(inv_ready, b + 1)
                for n in range(RT):
                    op = nc.vector.tensor_scalar(expo[:, n, :], expo[:, n, :], inv_sum[:, n:n + 1], None, ALU.mult)
                op.then_inc(attn_ready, 1)

            def attn_low(b, c):
                dve.wait_ge(ahi_ready, KC * b + c + 1)
                nc.vector.tensor_tensor(attnT[:, LO, c, :], att_bank(b, "attn", c)[:, :], attnT[:, HI, c, :],
                                        ALU.subtract).then_inc(alo_ready, 1)

            def add_mix(b, i):
                dve.wait_ge(mix_done, RT * b + i + 1)
                nc.vector.scalar_tensor_tensor(out=row_tile(b, i), in0=att_bank(b, "mix", i)[:, :],
                                               scalar=1.0 / ATT_SCALE, in1=row_tile(b, i),
                                               op0=ALU.mult, op1=ALU.add).then_inc(added, 1)

            def h_low(b, c):
                dve.wait_ge(hhi_ready, KC * b + c + 1)
                cols = bass.ds(b * S, S)
                nc.vector.tensor_tensor(hT[:, LO, c, cols], att_bank(b, "h", c)[:, :], hT[:, HI, c, cols],
                                        ALU.subtract).then_inc(hlo_ready, 1)

            def step(op, b, k):
                op.then_inc(r_step, 1)
                dve.wait_ge(r_step, ROUTE_STEPS * b + k)

            def over_tile(a):
                return a[:, :].unsqueeze(2).broadcast_to([P, RT, E])

            def read_logits(b):
                dve.wait_ge(logits_done, b + 1)
                parts = att_bank(b, "logits", 0)[:, 0:RT * 3 * NL].rearrange("p (t a e) -> p t e a", t=RT, a=3)
                nc.vector.tensor_reduce(logits[:, :, :], parts, AX.X, ALU.add).then_inc(logits_read, 1)
                dve.wait_ge(logits_read, b + 1)
                step(nc.vector.tensor_reduce(top[:, :], logits[:, :, 0:E], AX.X, ALU.max), b, 1)
                nc.vector.tensor_scalar(exp_in[:, :, E], logits[:, :, E], -1.0, None, ALU.mult)
                nc.vector.tensor_tensor(exp_in[:, :, 0:E], logits[:, :, 0:E], over_tile(top),
                                        ALU.subtract).then_inc(exp_in_ready, 1)

            def route(b):
                dve.wait_ge(r_exp, b + 1)
                nc.vector.tensor_scalar(gate_den[:, :], exp_out[:, :, E], 1.0, None, ALU.add)
                step(nc.vector.tensor_reduce(soft_sum[:, :], exp_out[:, :, 0:E], AX.X, ALU.add), b, 2)
                nc.vector.reciprocal(gate_val[:, :], gate_den[:, :])
                step(nc.vector.reciprocal(soft_inv[:, :], soft_sum[:, :]), b, 3)
                nc.vector.tensor_copy(combine[:, :, E:NC],
                                      gate_val[:, :].unsqueeze(2).broadcast_to([P, RT, NC - E]))
                step(nc.vector.tensor_tensor(probs[:, :, :], exp_out[:, :, 0:E], over_tile(soft_inv), ALU.mult), b, 4)
                for i in range(RT):
                    p_other = probs[:, i, :].unsqueeze(1).broadcast_to([P, E, E])
                    p_own = probs[:, i, :].unsqueeze(2).broadcast_to([P, E, E])
                    nc.vector.tensor_tensor(greater[:, i, :, :], p_other, p_own, ALU.is_gt)
                    op = nc.vector.tensor_tensor(equal[:, i, :, :], p_other, p_own, ALU.is_equal)
                step(op, b, 5)
                step(nc.vector.tensor_tensor(equal.rearrange("p t e j -> p t (e j)"),
                                             equal.rearrange("p t e j -> p t (e j)"),
                                             before[:, :, :].rearrange("p e j -> p (e j)").unsqueeze(1)
                                             .broadcast_to([P, RT, E * E]), ALU.mult), b, 6)
                step(nc.vector.tensor_tensor(greater.rearrange("p t e j -> p (t e j)"),
                                             greater.rearrange("p t e j -> p (t e j)"),
                                             equal.rearrange("p t e j -> p (t e j)"), ALU.add), b, 7)
                step(nc.vector.tensor_reduce(rank[:, :, :], greater, AX.X, ALU.add), b, 8)
                step(nc.vector.scalar_tensor_tensor(out=rank[:, :, :], in0=rank[:, :, :], scalar=TOP_K - 0.5,
                                                    in1=probs[:, :, :], op0=ALU.is_lt, op1=ALU.mult), b, 9)
                step(nc.vector.tensor_reduce(top_sum[:, :], rank[:, :, :], AX.X, ALU.add), b, 10)
                step(nc.vector.reciprocal(top_inv[:, :], top_sum[:, :]), b, 11)
                nc.vector.tensor_tensor(combine[:, :, 0:E], rank[:, :, :], over_tile(top_inv),
                                        ALU.mult).then_inc(combine_ready, 1)

            def combine_out(b):
                dve.wait_ge(combine_turned, b + 1)
                if not isinstance(b, int):
                    dve.wait_ge(combine_stored, 16 * b)
                nc.vector.tensor_copy(combineT[:, :], att_bank(b, "combine", 0)[0:NC, :]).then_inc(combineT_ready, 1)

            dve.sem_inc(silu_ready, PRIME)
            dve.sem_inc(prod_ready, PRIME)
            dve.sem_inc(down_done, PRIME)
            dve.sem_inc(block_summed, PRIME)

            dve.wait_ge(x0_loaded, 16)
            statistics(0, 0)
            normalize(0, 0)
            gw_ps = bank[3][:, 0:KC * NL].rearrange("p (k e) -> p k e", k=KC)
            dve.wait_ge(gw_turned, 1)
            nc.vector.tensor_copy(gw3[:, :, 0, :], gw_ps).then_inc(gw_step, 1)
            dve.wait_ge(gw_step, 1)
            nc.vector.tensor_tensor(gw_rest[:, 0, :, :], gw_ps, gw3[:, :, 0, :], ALU.subtract).then_inc(gw_step, 1)
            dve.wait_ge(gw_step, 2)
            nc.vector.tensor_copy(gw3[:, :, 1, :], gw_rest[:, 0, :, :]).then_inc(gw_step, 1)
            dve.wait_ge(gw_step, 3)
            nc.vector.tensor_tensor(gw_rest[:, 1, :, :], gw_rest[:, 0, :, :], gw3[:, :, 1, :],
                                    ALU.subtract).then_inc(gw_step, 1)
            dve.wait_ge(gw_step, 4)
            nc.vector.tensor_copy(gw3[:, :, 2, :], gw_rest[:, 1, :, :]).then_inc(gw_step, 1)
            for n in range(RT):
                row_max(0, n)
            scale_attn(0)
            for c in range(KC):
                x_low(0, c)
            for c in range(KC):
                attn_low(0, c)
            for i in range(RT):
                add_mix(0, i)
            statistics(1, 0)
            normalize(1, 0)
            for c in range(KC):
                h_low(0, c)
            dve.wait_ge(consts_ready, 3)
            read_logits(0)
            route(0)
            combine_out(0)
            dve.wait_ge(x_rest_loaded, 16)

            def attention(j, point, b):
                for stage, i in AT_POINT.get((j, point), ()):
                    if stage == "stats1":
                        statistics(0, b)
                    elif stage == "norm1":
                        normalize(0, b)
                    elif stage == "energy":
                        row_max(b, i)
                    elif stage == "scale":
                        scale_attn(b)
                    elif stage == "x":
                        x_low(b, i)
                    elif stage == "attn":
                        attn_low(b, i)
                    elif stage == "mix":
                        add_mix(b, i)
                    elif stage == "stats2":
                        statistics(1, b)
                    elif stage == "norm2":
                        normalize(1, b)
                    elif stage == "h":
                        h_low(b, i)
                    elif stage == "logits":
                        read_logits(b)
                    elif stage == "route":
                        route(b)
                    elif stage == "combine":
                        combine_out(b)

            def ffn_block(n, t, b=None):
                def beside(j, point):
                    if b is not None:
                        attention(j, point, b)

                for j in range(UT):
                    beside(j, "start")
                    beside(j, "gate")
                    dve.wait_ge(up_done, n * UT + j + 1)
                    dve.wait_ge(silu_ready, n * UT + PRIME + j + 1)
                    if j > 0:
                        dve.wait_ge(hid_lo, n * UT + j)
                    nc.vector.tensor_tensor(prod[:, :], silu_sb[:, :], up_ps[:, :], ALU.mult).then_inc(prod_ready, 1)
                    dve.wait_ge(prod_ready, n * UT + PRIME + j + 1)
                    if j == 0:
                        dve.wait_ge(combine_loaded, n * 16 + 16)
                    for p0, p1, e in pieces[j]:
                        for a, z in legal(p0, p1):
                            op = nc.vector.tensor_tensor(prod[a:z, :], prod[a:z, :], combine_b[a:z, e, :], ALU.mult)
                    op.then_inc(scaled, 1)
                    beside(j, "up")
                    dve.wait_ge(hid_hi, n * UT + j + 1)
                    nc.vector.tensor_tensor(hidden[:, j % 3, LO, :], prod[:, :], hidden[:, j % 3, HI, :],
                                            ALU.subtract).then_inc(hid_lo, 1)
                    beside(j, "down")
                dve.wait_ge(down_done, n * UT + PRIME + UT)
                for i in range(RT):
                    op = nc.vector.tensor_tensor(row_tile(t, i), out_ps[i][:, :], row_tile(t, i), ALU.add)
                op.then_inc(block_summed, 1)

            with dve.Fori(0, B - 1) as t:
                ffn_block(t, t, t + 1)
            with dve.Fori(B - 1, NG * B) as n:
                ffn_block(n, n % B)

        @block.tensor
        def _(pe):
            def turn_context(b, c):
                if c == 0:
                    pe.wait_ge(ctx_loaded, 16 * b + 16)
                if not isinstance(b, int):
                    pe.wait_ge((logits_read, combineT_ready)[c], b)
                for i in range(RT):
                    op = nc.tensor.transpose(att_bank(b, "ctx", c)[:, i * P:(i + 1) * P],
                                             ctx_sb[:, i, c * P:(c + 1) * P], ident[:, :])
                op.then_inc(turned, 1)

            def project(b, i):
                pe.wait_ge(ctxT_ready, CC * b + CC)
                for c in range(CC):
                    op = nc.tensor.matmul(att_bank(b, "qk", i)[:, :], wqkT[:, i, c, :], ctxT[:, c, :],
                                          start=(c == 0), stop=(c == CC - 1))
                op.then_inc(qk_done, 1)

            def energy(b, n):
                if n == 0:
                    pe.wait_ge(qk_ready, 2 * b + 2)
                elif n >= 2 and not isinstance(b, int):
                    pe.wait_ge(exp_done, RT * b + n - 1)
                nc.tensor.matmul(att_bank(b, "energy", n)[:, :], qT[:, n * P:(n + 1) * P], kT,
                                 start=True, stop=True).then_inc(energy_done, 1)

            def turn_x(b, c):
                if c == 0:
                    pe.wait_ge(normed_ready[0], b + 1)
                if not isinstance(b, int):
                    if c < 2:
                        pe.wait_ge(exp_done, RT * b + c + 3)
                    else:
                        pe.wait_ge(xlo_ready, KC * b + c - 1)
                for i in range(RT):
                    op = nc.tensor.transpose(att_bank(b, "x", c)[:, i * P:(i + 1) * P],
                                             normed[:, i, c * P:(c + 1) * P], ident[:, :])
                op.then_inc(turned, 1)

            def turn_attn(b, c):
                if c == 0:
                    pe.wait_ge(attn_ready, b + 1)
                if not isinstance(b, int):
                    if c < 2:
                        pe.wait_ge(xlo_ready, KC * b + c + 3)
                    else:
                        pe.wait_ge(alo_ready, KC * b + c - 1)
                for m in range(RT):
                    op = nc.tensor.transpose(att_bank(b, "attn", c)[:, m * P:(m + 1) * P],
                                             expo[:, m, c * P:(c + 1) * P], ident[:, :])
                op.then_inc(turned, 1)

            def mix(b, i):
                if i == 0:
                    pe.wait_ge(xlo_ready, KC * b + KC)
                    pe.wait_ge(alo_ready, RT * b + RT)
                elif i >= 2 and not isinstance(b, int):
                    pe.wait_ge(added, RT * b + i - 1)
                for c in range(KC):
                    for s, (xp, ap) in enumerate(PAIRS):
                        op = nc.tensor.matmul(att_bank(b, "mix", i)[:, :], xnT[:, xp, c, i * P:(i + 1) * P],
                                              attnT[:, ap, c, :], start=(c == 0 and s == 0),
                                              stop=(c == KC - 1 and s == len(PAIRS) - 1))
                op.then_inc(mix_done, 1)

            def turn_h(b, c):
                if c == 0:
                    pe.wait_ge(normed_ready[1], b + 1)
                elif c >= 2 and not isinstance(b, int):
                    pe.wait_ge(hlo_ready, KC * b + c - 1)
                for i in range(RT):
                    op = nc.tensor.transpose(att_bank(b, "h", c)[:, i * P:(i + 1) * P],
                                             normed[:, i, c * P:(c + 1) * P], ident[:, :])
                op.then_inc(turned, 1)

            def router_logits(b):
                pe.wait_ge(hlo_ready, KC * b + KC)
                for i in range(RT):
                    for c in range(KC):
                        for part in (HI, LO):
                            op = nc.tensor.matmul(att_bank(b, "logits", 0)[:, i * 3 * NL:(i + 1) * 3 * NL],
                                                  hT[:, part, c, bass.ds(b * S + i * P, P)],
                                                  gw3[:, c, :, :].rearrange("p a e -> p (a e)"),
                                                  start=(c == 0 and part == HI), stop=(c == KC - 1 and part == LO))
                op.then_inc(logits_done, 1)

            def turn_combine(b):
                pe.wait_ge(combine_ready, b + 1)
                for i in range(RT):
                    op = nc.tensor.transpose(att_bank(b, "combine", 0)[0:NC, i * P:(i + 1) * P],
                                             combine[:, i, :], ident[:, :])
                op.then_inc(combine_turned, 1)

            pe.wait_ge(consts_ready, 3)
            pe.wait_ge(wqk_loaded, 64)
            for i in range(2):
                for c in range(CC):
                    op = nc.tensor.transpose(bank[2][:, (i * CC + c) * P:(i * CC + c + 1) * P],
                                             wqk[:, i, c * P:(c + 1) * P], ident[:, :])
            op.then_inc(wqk_turned, 1)
            for c in range(CC):
                turn_context(0, c)
            pe.wait_ge(gw_loaded, 32)
            for c in range(KC):
                op = nc.tensor.transpose(bank[3][:, c * NL:(c + 1) * NL], gw_rows[:, c * P:(c + 1) * P],
                                         ident[0:NL, 0:NL])
            op.then_inc(gw_turned, 1)
            pe.wait_ge(wqkT_ready, 1)
            project(0, 0)
            pe.wait_ge(gw_step, 5)
            project(0, 1)
            for n in range(RT):
                energy(0, n)
            for c in range(KC):
                turn_x(0, c)
            for c in range(KC):
                turn_attn(0, c)
            for i in range(RT):
                mix(0, i)
            for c in range(KC):
                turn_h(0, c)
            router_logits(0)
            turn_combine(0)

            def attention(j, point, b):
                for stage, i in AT_POINT.get((j, point), ()):
                    if stage == "ctx":
                        turn_context(b, i)
                    elif stage == "qk":
                        project(b, i)
                    elif stage == "energy":
                        energy(b, i)
                    elif stage == "x":
                        turn_x(b, i)
                    elif stage == "attn":
                        turn_attn(b, i)
                    elif stage == "mix":
                        mix(b, i)
                    elif stage == "h":
                        turn_h(b, i)
                    elif stage == "logits":
                        router_logits(b)
                    elif stage == "combine":
                        turn_combine(b)

            def ffn_block(n, g, t, b=None):
                def product(kind, j, ps):
                    for c in range(KC):
                        for s, (wp, hp) in enumerate(PAIRS):
                            op = nc.tensor.matmul(ps[:, :], weights[:, j, wp, kind, c * P:(c + 1) * P],
                                                  hT[:, hp, c, bass.ds(t * S, S)], start=(c == 0 and s == 0),
                                                  stop=(c == KC - 1 and s == len(PAIRS) - 1))
                    return op

                def down(j):
                    pe.wait_ge(hid_lo, n * UT + j + 1)
                    if j == 0:
                        pe.wait_ge(block_summed, n + PRIME)
                    for i in range(RT):
                        for s, (hp, wp) in enumerate(PAIRS):
                            op = nc.tensor.matmul(out_ps[i][:, :], hidden[:, j % 3, hp, i * P:(i + 1) * P],
                                                  weights[:, j, wp, DOWN, :], start=(j == 0 and s == 0),
                                                  stop=(j == UT - 1 and s == len(PAIRS) - 1))
                    op.then_inc(down_done, 1)

                def beside(j, point):
                    if b is not None:
                        attention(j, point, b)

                for j in range(UT):
                    pe.wait_ge(split, g * UT + j + 1)
                    pe.wait_ge(silu_ready, n * UT + PRIME + j)
                    product(GATE, j, gate_ps).then_inc(gate_done, 1)
                    beside(j, "gate")
                    pe.wait_ge(prod_ready, n * UT + PRIME + j)
                    product(UP, j, up_ps).then_inc(up_done, 1)
                    beside(j, "up")
                    if j >= 2:
                        down(j - 2)
                    beside(j, "down")
                for j in range(UT - 2, UT):
                    down(j)

            with pe.Fori(0, B - 1) as t:
                ffn_block(t, 0, t, t + 1)
            with pe.Fori(B - 1, NG * B) as n:
                ffn_block(n, n // B, n % B)


_INS = ["x", "ctx_1024", "L0_xattn_Wq", "L0_xattn_bq", "L0_xattn_Wk", "L0_xattn_bk", "L0_ffn_gate_w",
        "L0_ffn_w_gate", "L0_ffn_w_up", "L0_ffn_w_down", "L0_ffn_sw_gate", "L0_ffn_sw_up", "L0_ffn_sw_down",
        "L0_ffn_shared_gate_w"]


def kernel(**inputs):
    import numpy as np
    import concourse.bacc as bacc
    from concourse.bass_utils import run_bass_kernel_spmd

    nc = bacc.Bacc("TRN2", target_bir_lowering=False, num_devices=1)
    arrays, args = {}, []
    for name in _INS:
        a = np.ascontiguousarray(inputs[name])
        arrays[name] = a
        args.append(nc.dram_tensor(name, a.shape, mybir.dt.from_np(a.dtype), kind="ExternalInput").ap())
    shape = inputs["x"].shape
    out = nc.dram_tensor("out", shape, F32, kind="ExternalOutput").ap()
    combine_dram = nc.dram_tensor("combine_dram", (12, shape[0] * shape[1]), F32, kind="Internal").ap()
    build_xattn_moe(nc, *args, out, combine_dram)
    r = run_bass_kernel_spmd(nc, [arrays], core_ids=[0])
    return r.results[0]["out"]
```

```python
from contextlib import ExitStack

import concourse.bass as bass
from concourse import mybir

ALU = mybir.AluOpType
ACT = mybir.ActivationFunctionType
AX = mybir.AxisListType
F32 = mybir.dt.float32
F16 = mybir.dt.float16
BF16 = mybir.dt.bfloat16

P = 128
HI, LO = 0, 1
PAIRS = ((HI, HI), (HI, LO), (LO, HI))
TOP_K = 2
EARLY = 5
AT_POINT = {
    (0, "start"): [("load", 0)],
    (0, "up"): [("combine", 0), ("ctx", 0)],
    (0, "down"): [("stats1", 0)],
    (1, "gate"): [("ctx", 1)],
    (1, "up"): [("qk", 0)],
    (2, "gate"): [("qk", 1)],
    (2, "up"): [("energy", 0)],
    (2, "down"): [("energy", 1), ("norm1", 0)],
    (3, "gate"): [("energy", 2)],
    (3, "up"): [("energy", 3)],
    (3, "down"): [("x", 0), ("scale", 0)],
    (4, "gate"): [("x", 1)],
    (4, "up"): [("x", 2)],
    (4, "down"): [("x", 3)],
    (5, "gate"): [("attn", 0)],
    (5, "up"): [("attn", 1)],
    (5, "down"): [("attn", 2)],
    (6, "gate"): [("attn", 3)],
    (6, "up"): [("mix", 0)],
    (6, "down"): [("mix", 1)],
    (7, "gate"): [("mix", 2)],
    (7, "up"): [("mix", 3)],
    (7, "down"): [("stats2", 0)],
    (8, "start"): [("norm2", 0)],
    (8, "up"): [("h", 0)],
    (8, "down"): [("h", 1)],
    (9, "gate"): [("h", 2)],
    (9, "up"): [("h", 3)],
    (10, "down"): [("logits", 0), ("route", 0)],
}
AT_POINT_FIRST = {
    (0, "gate"): [("logits_before", 0)],
    (0, "up"): [("x_low", 0)],
    (1, "gate"): [("combine", 0), ("attn_low", 0)],
    (1, "up"): [("attn", 0), ("attn", 1), ("attn", 2), ("attn", 3)],
    (2, "gate"): [("mix", 0), ("mix", 1), ("mix", 2), ("mix", 3)],
    (2, "up"): [("stats2", 0)],
    (3, "gate"): [("norm2", 0)],
    (3, "down"): [("h", 0)],
    (4, "gate"): [("h", 1)],
    (4, "up"): [("h", 2)],
    (4, "down"): [("h", 3)],
    (5, "up"): [("logits", 0)],
    (5, "down"): [("route", 0)],
}
WARM_UP = 16
ROUTE_STEPS = 11
GATE, UP, DOWN = 0, 1, 2


def written_out(b):
    return isinstance(b, int)


def build_xattn_moe(nc, x, ctx_in, w_q, b_q, w_k, b_k, gate_w, w_gate, w_up, w_down,
                    sw_gate, sw_up, sw_down, shared_gate_w, out, combine_dram):
    B, S, H = x.shape
    C = ctx_in.shape[2]
    E, _, I = w_gate.shape
    IS = sw_gate.shape[1]
    D = w_q.shape[0]
    RT = S // P
    KC = H // P
    CC = C // P
    EG = IS // I
    NG = E // EG + 1
    UT = IS // P
    NL = E + 1
    NC = NG * EG
    assert D == P and S == H and EG * I == IS and UT * P == IS and E % EG == 0
    EPS = 1e-5
    ATT_SCALE = 1024.0

    BORROWED = UT - 4

    pieces = []
    for j in range(UT):
        cut, at = [], j * P
        while at < (j + 1) * P:
            e = at // I
            end = min((e + 1) * I, (j + 1) * P)
            cut.append((at - j * P, end - j * P, e))
            at = end
        pieces.append(cut)

    def legal(p0, p1):
        while p0 < p1:
            most = {0: 128, 32: 32, 64: 64, 96: 32}[p0]
            yield p0, min(p1, p0 + most)
            p0 = min(p1, p0 + most)

    with ExitStack() as stack:
        def sb(name, shape, dt):
            return stack.enter_context(nc.sbuf_tensor(name, shape, dt))

        def sem(name):
            return stack.enter_context(nc.semaphore(name))

        bank = [stack.enter_context(nc.psum_tensor(f"bank{i}", [P, 512], F32)) for i in range(8)]
        gate_ps, up_ps, out_ps = bank[2], bank[3], bank[4:8]

        def four_banks(b, stage):
            return written_out(b) and (b == 0 or stage not in ("h", "logits")) and stage != "combine"

        def att_bank(b, stage, i):
            if stage == "h" and four_banks(b, stage):
                return bank[(2, 0, 1, 3)[i]]
            if four_banks(b, stage):
                return bank[b * 4 + (2 if stage == "qk" else 0) + i]
            return bank[1] if stage == "combine" else bank[i % 2]

        rows = sb("rows", [P, B * RT * H], F32)
        hT = sb("hT", [P, 2, KC, B * S], F16)
        weights = sb("weights", [P, UT, 2, 3, 512], BF16)
        staging = sb("staging", [P, 2, 3, 512], F32)
        ctx_sb = sb("ctx_sb", [P, RT, C], F32)
        normed = sb("normed", [P, RT, H], F32)
        xnT = sb("xnT", [P, 2, KC, S], F16)
        expo = sb("expo", [P, RT, S], F32)
        combineT = sb("combineT", [NC, S], F32)
        attn_space = sb("attn_space", [P, 2 * RT * S], F16)
        combine_b = sb("combine_b", [P, EG, S], F32)
        silu_sb = sb("silu_sb", [P, S], F32)
        prod = sb("prod", [P, 2, S], F32)
        hidden = sb("hidden", [P, 3, 2, S], BF16)

        class AttentionPlace:
            def __init__(self, ctx_rows, normed, xnT, expo, attn_space):
                self.ctx_rows, self.normed, self.xnT, self.expo = ctx_rows, normed, xnT, expo
                self.attnT = attn_space.rearrange("p (a t n) -> p a t n", a=2, t=RT)
                front = attn_space.bitcast(F32)
                self.ctxT = front[:, 0:CC * S].rearrange("p (c n) -> p c n", c=CC)
                self.qT = front[:, CC * S:CC * S + S]
                self.kT = front[:, CC * S + S:CC * S + 2 * S]

        own_place = AttentionPlace(ctx_sb[:, :, :], normed[:, :, :], xnT[:, :, :, :], expo[:, :, :],
                                   attn_space[:, :])
        last_tiles = weights[:, BORROWED:UT].rearrange("p j a k u -> p (j a k u)")
        third = 2 * RT * S
        borrowed_place = AttentionPlace(
            prod[:, :, :].rearrange("p a (t c) -> p (a t) c", c=C),
            last_tiles[:, 0:third].bitcast(F32).rearrange("p (t h) -> p t h", t=RT),
            last_tiles[:, third:2 * third].bitcast(F16).rearrange("p (a c s) -> p a c s", a=2, c=KC),
            combine_b[:, :, :],
            last_tiles[:, 2 * third:3 * third].bitcast(F16))

        def place(b):
            return borrowed_place if written_out(b) and b == 1 else own_place

        wqk = sb("wqk", [P, 2, C], F32)
        wqkT = sb("wqkT", [P, 2, CC, P], F32)
        bqk = sb("bqk", [P, 2], F32)
        gw_rows = combineT[0:NL, :]
        gw_rest = sb("gw_rest", [P, 2, KC, NL], F32)
        gw3 = sb("gw3", [P, KC, 3, NL], BF16)
        ident = sb("ident", [P, P], F32)
        before = sb("before", [P, E, E], F32)
        minus_half = sb("minus_half", [P, RT], F32)
        stats = sb("stats", [P, 2, RT, 6], F32)
        mean_var = sb("mean_var", [P, 2, RT, 2], F32)
        var_eps = sb("var_eps", [P, 2, RT], F32)
        rstd = sb("rstd", [P, 2, RT], F32)
        neg_max = sb("neg_max", [P, RT], F32)
        exp_sum = sb("exp_sum", [P, RT], F32)
        sum_scaled = sb("sum_scaled", [P, RT], F32)
        inv_sum = sb("inv_sum", [P, RT], F32)
        logits = sb("logits", [P, RT, NL], F32)
        top = sb("top", [P, RT], F32)
        exp_in = sb("exp_in", [P, RT, NL], F32)
        exp_out = sb("exp_out", [P, RT, NL], F32)
        soft_sum = sb("soft_sum", [P, RT], F32)
        soft_inv = sb("soft_inv", [P, RT], F32)
        probs = sb("probs", [P, RT, E], F32)
        compared = wqk[:, :, :].rearrange("p a (t e j) -> p a t e j", t=RT, e=E)
        greater, equal = compared[:, 0], compared[:, 1]
        rank = sb("rank", [P, RT, E], F32)
        top_sum = sb("top_sum", [P, RT], F32)
        top_inv = sb("top_inv", [P, RT], F32)
        gate_den = sb("gate_den", [P, RT], F32)
        gate_val = sb("gate_val", [P, RT], F32)
        combine = sb("combine", [P, RT, NC], F32)
        carrier = sb("carrier", [P, 2], F32)

        x0_loaded, x1_loaded, x_rest_loaded = sem("x0_loaded"), sem("x1_loaded"), sem("x_rest_loaded")
        ctx_loaded = sem("ctx_loaded")
        ctx1_loaded = sem("ctx1_loaded")
        wqk_loaded, bqk_loaded, gw_loaded = sem("wqk_loaded"), sem("bqk_loaded"), sem("gw_loaded")
        staged = [sem("staged0"), sem("staged1")]
        combine_stored = sem("combine_stored")
        combine_loaded = [sem(f"combine_loaded{e}") for e in range(EG)]
        out_stored = sem("out_stored")
        consts_zeroed, consts_ready = sem("consts_zeroed"), sem("consts_ready")
        wqk_turned, wqkT_ready = sem("wqk_turned"), sem("wqkT_ready")
        gw_turned, gw_step = sem("gw_turned"), sem("gw_step")
        stats_done, aggr_done = [sem("stats_done1"), sem("stats_done2")], [sem("aggr_done1"), sem("aggr_done2")]
        var_ready, rstd_ready = [sem("var_ready1"), sem("var_ready2")], [sem("rstd_ready1"), sem("rstd_ready2")]
        normed_ready = [sem("normed_ready1"), sem("normed_ready2")]
        ctx_turned, x_turned, attn_turned, h_turned = (sem("ctx_turned"), sem("x_turned"),
                                                       sem("attn_turned"), sem("h_turned"))
        ctxT_ready, qk_done, qk_ready = sem("ctxT_ready"), sem("qk_done"), sem("qk_ready")
        xhi_ready, xlo_ready = sem("xhi_ready"), sem("xlo_ready")
        energy_done, max_ready, exp_done = sem("energy_done"), sem("max_ready"), sem("exp_done")
        sum_ready, inv_ready = sem("sum_ready"), sem("inv_ready")
        attn_ready = sem("attn_ready")
        ahi_ready, alo_ready = sem("ahi_ready"), sem("alo_ready")
        mix_done, added = sem("mix_done"), sem("added")
        hhi_ready, hlo_ready = sem("hhi_ready"), sem("hlo_ready")
        logits_done, logits_read = sem("logits_done"), sem("logits_read")
        r_step, exp_in_ready, r_exp = sem("r_step"), sem("exp_in_ready"), sem("r_exp")
        combine_ready, combine_turned = sem("combine_ready"), sem("combine_turned")
        combineT_ready = sem("combineT_ready")
        high_split, split = sem("high_split"), sem("split")
        gate_done, up_done, down_done = sem("gate_done"), sem("up_done"), sem("down_done")
        silu_ready, prod_ready = sem("silu_ready"), sem("prod_ready")
        scaled, hid_hi, hid_lo = sem("scaled"), sem("hid_hi"), sem("hid_lo")
        out_done, block_summed = sem("out_done"), sem("block_summed")

        PRIME = 1

        def row_tile(b, i):
            return rows[:, bass.ds((b * RT + i) * H, H)]

        block = stack.enter_context(nc.Block())

        @block.sync
        def _(sp):
            rows_t = rows[:, :].rearrange("p (t h) -> p t h", h=H)

            def load_rows(b0, b1, x_sem):
                sp.dma_start(rows_t[:, b0 * RT:b1 * RT, :],
                             x[b0:b1].rearrange("b (t p) h -> p (b t) h", p=P)).then_inc(x_sem, 16)

            def load_unit_tile(g, j):
                n = g * UT + j
                if n >= 2:
                    sp.wait_ge(split, n - 1)
                slot = n % 2
                if g < NG - 1:
                    for kind, w in ((GATE, w_gate), (UP, w_up)):
                        dst = staging[:, slot, kind, :].rearrange("p (k u) -> p k u", k=KC)
                        for p0, p1, e in pieces[j]:
                            u0 = j * P + p0 - e * I
                            src = w[g * EG + e, :, u0:u0 + p1 - p0].rearrange("(k p) u -> p k u", p=P)
                            sp.dma_start(dst[:, :, p0:p1], src).then_inc(staged[slot], 16)
                    src = w_down.rearrange("e i h -> (e i) h")[(g * UT + j) * P:(g * UT + j + 1) * P, :]
                else:
                    for kind, w in ((GATE, sw_gate), (UP, sw_up)):
                        sp.dma_start(staging[:, slot, kind, :].rearrange("p (k u) -> p k u", k=KC),
                                     w[:, j * P:(j + 1) * P].rearrange("(k p) u -> p k u", p=P)
                                     ).then_inc(staged[slot], 16)
                    src = sw_down[j * P:(j + 1) * P, :]
                sp.dma_start(staging[:, slot, DOWN, :], src).then_inc(staged[slot], 16)

            def load_group(g):
                for j in range(UT):
                    load_unit_tile(g, j)

            def share_combine(b):
                sp.wait_ge(combineT_ready, b + 1)
                sp.dma_start(combine_dram[:, b * S:(b + 1) * S], combineT[:, :]).then_inc(combine_stored, 16)
                sp.wait_ge(combine_stored, 16 * (b + 1))

            def load_combine(g, t):
                n = g * B + t
                if n:
                    sp.wait_ge(scaled, UT * n)
                else:
                    sp.wait_ge(attn_turned, KC * 2)
                for e in range(EG):
                    src = combine_dram[g * EG + e, t * S:(t + 1) * S]
                    sp.dma_start(combine_b[:, e, :], src.partition_broadcast(P)).then_inc(combine_loaded[e], 16)

            sp.dma_start(wqk[:, 0, :], w_q).then_inc(wqk_loaded, 16)
            sp.dma_start(wqk[:, 1, :], w_k).then_inc(wqk_loaded, 16)
            load_rows(0, 1, x0_loaded)
            sp.dma_start(bqk[:, 0:1], b_q.rearrange("(p a) -> p a", a=1)).then_inc(bqk_loaded, 16)
            sp.dma_start(bqk[:, 1:2], b_k.rearrange("(p a) -> p a", a=1)).then_inc(bqk_loaded, 16)
            sp.dma_start(gw_rows[0:E, :], gate_w).then_inc(gw_loaded, 16)
            sp.dma_start(gw_rows[E:NL, :], shared_gate_w.rearrange("h a -> a h")).then_inc(gw_loaded, 16)
            sp.dma_start(place(1).ctx_rows, ctx_in[1].rearrange("(t p) c -> p t c", p=P)).then_inc(ctx1_loaded, 16)
            load_rows(1, 2, x1_loaded)
            load_unit_tile(0, 0)
            load_unit_tile(0, 1)
            load_rows(2, B, x_rest_loaded)
            for j in range(2, EARLY):
                load_unit_tile(0, j)
            share_combine(0)
            load_combine(0, 0)
            for j in range(EARLY, UT):
                load_unit_tile(0, j)
            for t in range(1, B):
                share_combine(t)
                load_combine(0, t)
            for g in range(1, NG):
                for j in range(UT - 2):
                    load_unit_tile(g, j)
                load_combine(g, 0)
                for j in range(UT - 2, UT):
                    load_unit_tile(g, j)
                for t in range(1, B):
                    load_combine(g, t)
            for t in range(B):
                for i in range(RT):
                    sp.wait_ge(block_summed, PRIME + RT * (B * (NG - 1) + t) + i + 1)
                    sp.dma_start(out[t, i * P:(i + 1) * P, :], row_tile(t, i)).then_inc(out_stored, 16)
            sp.wait_ge(out_stored, 16 * B * RT)

        @block.gpsimd
        def _(pool):
            nc.gpsimd.memset(ident[:, :], 0.0).then_inc(consts_zeroed, 1)
            nc.gpsimd.memset(before[:, :, :], 1.0).then_inc(consts_zeroed, 1)
            nc.gpsimd.memset(minus_half[:, :], -0.5).then_inc(consts_ready, 1)
            pool.wait_ge(consts_zeroed, 2)
            nc.gpsimd.affine_select(out=ident[:, :], in_=ident[:, :], compare_op=ALU.not_equal, fill=1.0,
                                    base=0, pattern=[[-1, P]], channel_multiplier=1).then_inc(consts_ready, 1)
            nc.gpsimd.affine_select(out=before[:, :, :], in_=before[:, :, :], compare_op=ALU.is_gt, fill=0.0,
                                    base=0, pattern=[[1, E], [-1, E]], channel_multiplier=0).then_inc(consts_ready, 1)

            arrived = [0, 0]

            def split_unit_tile(g, j):
                slot = (g * UT + j) % 2
                n_dmas = 3 if g == NG - 1 else 1 + 2 * len(pieces[j])
                arrived[slot] += 16 * n_dmas
                pool.wait_ge(staged[slot], arrived[slot])
                if g > 0:
                    if j < UT - 1:
                        pool.wait_ge(down_done, PRIME + (UT - 1) * (B * g - 1) + j + 1)
                    else:
                        pool.wait_ge(block_summed, PRIME + RT * B * g)
                elif j == BORROWED:
                    pool.wait_ge(hlo_ready, KC * 2)
                nc.gpsimd.tensor_copy(weights[:, j, HI, :, :], staging[:, slot, :, :]).then_inc(high_split, 1)
                pool.wait_ge(high_split, g * UT + j + 1)
                nc.gpsimd.tensor_tensor(weights[:, j, LO, :, :], staging[:, slot, :, :], weights[:, j, HI, :, :],
                                        ALU.subtract).then_inc(split, 1)

            def inverse_deviation(which, b):
                pool.wait_ge(var_ready[which], b + 1)
                nc.gpsimd.tensor_tensor(rstd[:, which, :], var_eps[:, which, :], minus_half[:, :],
                                        ALU.pow).then_inc(rstd_ready[which], 1)

            pool.wait_ge(consts_ready, 3)
            inverse_deviation(0, 0)
            split_unit_tile(0, 0)
            inverse_deviation(0, 1)
            split_unit_tile(0, 1)
            inverse_deviation(1, 0)
            for j in range(2, 5):
                split_unit_tile(0, j)
            inverse_deviation(1, 1)
            for j in range(5, UT):
                split_unit_tile(0, j)
            for b in range(2, B):
                inverse_deviation(0, b)
                inverse_deviation(1, b)
            for g in range(1, NG):
                for j in range(UT):
                    split_unit_tile(g, j)

        @block.scalar
        def _(act):
            def load_context(b):
                src = ctx_in[0] if written_out(b) else ctx_in[bass.ds(b, 1)].rearrange("b s c -> (b s) c")
                act.dma_start(ctx_sb[:, :, :], src.rearrange("(t p) c -> p t c", p=P)).then_inc(ctx_loaded, 16)

            def context_turned(b, c):
                act.wait_ge(ctx_turned, CC * b + c + 1)
                nc.scalar.copy(place(b).ctxT[:, c, :], att_bank(b, "ctx", c)[:, :]).then_inc(ctxT_ready, 1)

            def project(b, i):
                act.wait_ge(qk_done, 2 * b + i + 1)
                nc.scalar.activation((place(b).qT, place(b).kT)[i], att_bank(b, "qk", i)[:, :], ACT.Identity,
                                     bias=bqk[:, i:i + 1]).then_inc(qk_ready, 1)

            def exponential(b, n):
                act.wait_ge(max_ready, RT * b + n + 1)
                nc.scalar.activation(place(b).expo[:, n, :], att_bank(b, "energy", n)[:, :], ACT.Exp,
                                     bias=neg_max[:, n:n + 1],
                                     accum_out=exp_sum[:, n:n + 1]).then_inc(exp_done, 1)

            def x_high(b, c):
                act.wait_ge(x_turned, KC * b + c + 1)
                nc.scalar.copy(place(b).xnT[:, HI, c, :], att_bank(b, "x", c)[:, :]).then_inc(xhi_ready, 1)

            def attn_high(b, c):
                act.wait_ge(attn_turned, KC * b + c + 1)
                nc.scalar.copy(place(b).attnT[:, HI, c, :], att_bank(b, "attn", c)[:, :]).then_inc(ahi_ready, 1)

            def h_high(b, c):
                act.wait_ge(h_turned, KC * b + c + 1)
                nc.scalar.copy(hT[:, HI, c, bass.ds(b * S, S)], att_bank(b, "h", c)[:, :]).then_inc(hhi_ready, 1)

            def router_exp(b):
                act.wait_ge(exp_in_ready, b + 1)
                nc.scalar.activation(exp_out[:, :, :], exp_in[:, :, :], ACT.Exp).then_inc(r_exp, 1)

            load_context(0)
            act.wait_ge(wqk_turned, 1)
            nc.scalar.copy(wqkT[:, :, :, :].rearrange("p a c d -> p (a c d)"),
                           bank[4][:, :]).then_inc(wqkT_ready, 1)
            for c in range(CC):
                context_turned(0, c)
            act.wait_ge(bqk_loaded, 32)
            for i in range(2):
                project(0, i)
            for c in range(CC):
                context_turned(1, c)
            exponential(0, 0)
            exponential(0, 1)
            x_high(0, 0)
            exponential(0, 2)
            x_high(0, 1)
            exponential(0, 3)
            x_high(0, 2)
            x_high(0, 3)
            for i in range(2):
                project(1, i)
            for c in range(KC):
                attn_high(0, c)
            for n in range(RT):
                exponential(1, n)
            x_high(1, 0)
            x_high(1, 1)
            for c in range(KC):
                h_high(0, c)
            x_high(1, 2)
            x_high(1, 3)

            def attention(j, point, b):
                for stage, i in (AT_POINT_FIRST if written_out(b) else AT_POINT).get((j, point), ()):
                    if stage == "load":
                        load_context(b)
                    elif stage == "ctx":
                        context_turned(b, i)
                    elif stage == "qk":
                        project(b, i)
                    elif stage == "energy":
                        exponential(b, i)
                    elif stage == "x":
                        x_high(b, i)
                    elif stage == "attn":
                        attn_high(b, i)
                    elif stage == "h":
                        h_high(b, i)
                    elif stage == "logits":
                        router_exp(b)
                    elif stage == "logits_before":
                        router_exp(b - 1)

            def ffn_block(n, b=None):
                def beside(j, point):
                    if b is not None:
                        attention(j, point, b)

                def high_part(j):
                    act.wait_ge(scaled, n * UT + j + 1)
                    act.wait_ge(down_done, n * (UT - 1) + PRIME + max(0, j - 2))
                    nc.scalar.copy(hidden[:, j % 3, HI, :], prod[:, j % 2, :]).then_inc(hid_hi, 1)

                for j in range(UT):
                    beside(j, "start")
                    act.wait_ge(gate_done, n * UT + j + 1)
                    act.wait_ge(prod_ready, n * UT + PRIME + j)
                    nc.scalar.activation(silu_sb[:, :], gate_ps[:, :], ACT.Silu).then_inc(silu_ready, 1)
                    beside(j, "gate")
                    beside(j, "up")
                    if j == 1:
                        high_part(0)
                    if j > 0:
                        high_part(j)
                    beside(j, "down")

            ffn_block(0, 1)
            with act.Fori(1, B - 1) as t:
                ffn_block(t, t + 1)
            with act.Fori(B - 1, NG * B) as n:
                ffn_block(n)

        @block.vector
        def _(dve):
            def statistics(which, b):
                if which == 1:
                    dve.wait_ge(added, RT * b + RT)
                    nc.vector.memset(carrier[:, 1:2], 0.0)
                for i in range(RT):
                    op = nc.vector.bn_stats(stats[:, which, i, :], row_tile(b, i))
                op.then_inc(stats_done[which], 1)
                variance(which, b)

            def variance(which, b):
                dve.wait_ge(stats_done[which], b + 1)
                if written_out(b) and b > 0:
                    dve.wait_ge(normed_ready[which], RT * b)
                nc.vector.memset(carrier[:, 0:1], 0.0)
                for i in range(RT):
                    op = nc.vector.bn_aggr(mean_var[:, which, i, :], stats[:, which, i, :])
                op.then_inc(aggr_done[which], 1)
                dve.wait_ge(aggr_done[which], b + 1)
                nc.vector.tensor_scalar(var_eps[:, which, :], mean_var[:, which, :, 1], EPS, None,
                                        ALU.add).then_inc(var_ready[which], 1)

            def normalize(which, b):
                dve.wait_ge(rstd_ready[which], b + 1)
                for i in range(RT):
                    op = nc.vector.tensor_scalar(place(b).normed[:, i, :], row_tile(b, i), mean_var[:, which, i, 0:1],
                                                 rstd[:, which, i:i + 1], ALU.subtract, ALU.mult)
                    op.then_inc(normed_ready[which], 1)

            def x_low(b, c):
                dve.wait_ge(xhi_ready, KC * b + c + 1)
                nc.vector.tensor_tensor(place(b).xnT[:, LO, c, :], att_bank(b, "x", c)[:, :],
                                        place(b).xnT[:, HI, c, :], ALU.subtract).then_inc(xlo_ready, 1)

            def row_max(b, n):
                dve.wait_ge(energy_done, RT * b + n + 1)
                nc.vector.tensor_reduce(neg_max[:, n:n + 1], att_bank(b, "energy", n)[:, :], AX.X, ALU.max,
                                        negate=True).then_inc(max_ready, 1)

            def scale_attn(b, n):
                one = slice(n, n + 1)
                dve.wait_ge(exp_done, RT * b + n + 1)
                nc.vector.tensor_scalar(sum_scaled[:, one], exp_sum[:, one], 1.0 / ATT_SCALE, None,
                                        ALU.mult).then_inc(sum_ready, 1)
                dve.wait_ge(sum_ready, RT * b + n + 1)
                nc.vector.reciprocal(inv_sum[:, one], sum_scaled[:, one]).then_inc(inv_ready, 1)
                dve.wait_ge(inv_ready, RT * b + n + 1)
                nc.vector.tensor_scalar(place(b).expo[:, n, :], place(b).expo[:, n, :], inv_sum[:, one], None,
                                        ALU.mult).then_inc(attn_ready, 1)

            def attn_low(b, c):
                dve.wait_ge(ahi_ready, KC * b + c + 1)
                nc.vector.tensor_tensor(place(b).attnT[:, LO, c, :], att_bank(b, "attn", c)[:, :],
                                        place(b).attnT[:, HI, c, :], ALU.subtract).then_inc(alo_ready, 1)

            def add_mix(b, i):
                dve.wait_ge(mix_done, RT * b + i + 1)
                nc.vector.scalar_tensor_tensor(out=row_tile(b, i), in0=att_bank(b, "mix", i)[:, :],
                                               scalar=1.0 / ATT_SCALE, in1=row_tile(b, i),
                                               op0=ALU.mult, op1=ALU.add).then_inc(added, 1)

            def h_low(b, c):
                dve.wait_ge(hhi_ready, KC * b + c + 1)
                cols = bass.ds(b * S, S)
                nc.vector.tensor_tensor(hT[:, LO, c, cols], att_bank(b, "h", c)[:, :], hT[:, HI, c, cols],
                                        ALU.subtract).then_inc(hlo_ready, 1)

            def step(op, b, k):
                op.then_inc(r_step, 1)
                dve.wait_ge(r_step, ROUTE_STEPS * b + k)

            def over_tile(a):
                return a[:, :].unsqueeze(2).broadcast_to([P, RT, E])

            def read_logits(b):
                dve.wait_ge(logits_done, b + 1)
                parts = att_bank(b, "logits", 0)[:, 0:RT * 3 * NL].rearrange("p (t a e) -> p t e a", t=RT, a=3)
                nc.vector.tensor_reduce(logits[:, :, :], parts, AX.X, ALU.add).then_inc(logits_read, 1)
                dve.wait_ge(logits_read, b + 1)
                step(nc.vector.tensor_reduce(top[:, :], logits[:, :, 0:E], AX.X, ALU.max), b, 1)
                nc.vector.tensor_scalar(exp_in[:, :, E], logits[:, :, E], -1.0, None, ALU.mult)
                nc.vector.tensor_tensor(exp_in[:, :, 0:E], logits[:, :, 0:E], over_tile(top),
                                        ALU.subtract).then_inc(exp_in_ready, 1)

            def route(b):
                dve.wait_ge(r_exp, b + 1)
                nc.vector.tensor_scalar(gate_den[:, :], exp_out[:, :, E], 1.0, None, ALU.add)
                step(nc.vector.tensor_reduce(soft_sum[:, :], exp_out[:, :, 0:E], AX.X, ALU.add), b, 2)
                nc.vector.reciprocal(gate_val[:, :], gate_den[:, :])
                step(nc.vector.reciprocal(soft_inv[:, :], soft_sum[:, :]), b, 3)
                nc.vector.tensor_copy(combine[:, :, E:NC],
                                      gate_val[:, :].unsqueeze(2).broadcast_to([P, RT, NC - E]))
                step(nc.vector.tensor_tensor(probs[:, :, :], exp_out[:, :, 0:E], over_tile(soft_inv), ALU.mult), b, 4)
                p_other = probs[:, :, :].unsqueeze(2).broadcast_to([P, RT, E, E])
                p_own = probs[:, :, :].unsqueeze(3).broadcast_to([P, RT, E, E])
                nc.vector.tensor_tensor(greater, p_other, p_own, ALU.is_gt)
                step(nc.vector.tensor_tensor(equal, p_other, p_own, ALU.is_equal), b, 5)
                step(nc.vector.tensor_tensor(equal.rearrange("p t e j -> p t (e j)"),
                                             equal.rearrange("p t e j -> p t (e j)"),
                                             before[:, :, :].rearrange("p e j -> p (e j)").unsqueeze(1)
                                             .broadcast_to([P, RT, E * E]), ALU.mult), b, 6)
                step(nc.vector.tensor_tensor(greater.rearrange("p t e j -> p (t e j)"),
                                             greater.rearrange("p t e j -> p (t e j)"),
                                             equal.rearrange("p t e j -> p (t e j)"), ALU.add), b, 7)
                step(nc.vector.tensor_reduce(rank[:, :, :], greater, AX.X, ALU.add), b, 8)
                step(nc.vector.scalar_tensor_tensor(out=rank[:, :, :], in0=rank[:, :, :], scalar=TOP_K - 0.5,
                                                    in1=probs[:, :, :], op0=ALU.is_lt, op1=ALU.mult), b, 9)
                step(nc.vector.tensor_reduce(top_sum[:, :], rank[:, :, :], AX.X, ALU.add), b, 10)
                step(nc.vector.reciprocal(top_inv[:, :], top_sum[:, :]), b, 11)
                nc.vector.tensor_tensor(combine[:, :, 0:E], rank[:, :, :], over_tile(top_inv),
                                        ALU.mult).then_inc(combine_ready, 1)

            def combine_out(b):
                dve.wait_ge(combine_turned, b + 1)
                nc.vector.tensor_copy(combineT[:, :], att_bank(b, "combine", 0)[0:NC, :]).then_inc(combineT_ready, 1)

            dve.sem_inc(silu_ready, PRIME)
            dve.sem_inc(prod_ready, PRIME)
            dve.sem_inc(down_done, PRIME)
            dve.sem_inc(block_summed, PRIME)

            dve.wait_ge(x0_loaded, 16)
            statistics(0, 0)
            gw_ps = bank[5][:, 0:KC * NL].rearrange("p (k e) -> p k e", k=KC)
            dve.wait_ge(gw_turned, 1)
            nc.vector.tensor_copy(gw3[:, :, 0, :], gw_ps).then_inc(gw_step, 1)
            dve.wait_ge(gw_step, 1)
            nc.vector.tensor_tensor(gw_rest[:, 0, :, :], gw_ps, gw3[:, :, 0, :], ALU.subtract).then_inc(gw_step, 1)
            dve.wait_ge(gw_step, 2)
            nc.vector.tensor_copy(gw3[:, :, 1, :], gw_rest[:, 0, :, :]).then_inc(gw_step, 1)
            dve.wait_ge(gw_step, 3)
            nc.vector.tensor_tensor(gw_rest[:, 1, :, :], gw_rest[:, 0, :, :], gw3[:, :, 1, :],
                                    ALU.subtract).then_inc(gw_step, 1)
            dve.wait_ge(gw_step, 4)
            nc.vector.tensor_copy(gw3[:, :, 2, :], gw_rest[:, 1, :, :]).then_inc(gw_step, 1)
            normalize(0, 0)
            row_max(0, 0)
            row_max(0, 1)
            scale_attn(0, 0)
            row_max(0, 2)
            scale_attn(0, 1)
            row_max(0, 3)
            scale_attn(0, 2)
            x_low(0, 0)
            scale_attn(0, 3)
            for c in range(1, KC):
                x_low(0, c)
            for c in range(KC):
                attn_low(0, c)
            dve.wait_ge(x1_loaded, 16)
            statistics(0, 1)
            row_max(1, 0)
            row_max(1, 1)

            def add_and_measure(i):
                add_mix(0, i)
                dve.wait_ge(added, i + 1)
                return nc.vector.bn_stats(stats[:, 1, i, :], row_tile(0, i))

            add_and_measure(0)
            normalize(0, 1)
            add_and_measure(1)
            add_and_measure(2)
            add_and_measure(3).then_inc(stats_done[1], 1)
            variance(1, 0)
            row_max(1, 2)
            row_max(1, 3)
            normalize(1, 0)
            scale_attn(1, 0)
            for c in range(KC):
                h_low(0, c)
            scale_attn(1, 1)
            scale_attn(1, 2)
            dve.wait_ge(consts_ready, 3)
            dve.wait_ge(x_rest_loaded, 16)

            def attention(j, point, b):
                for stage, i in (AT_POINT_FIRST if written_out(b) else AT_POINT).get((j, point), ()):
                    if stage == "stats1":
                        statistics(0, b)
                    elif stage == "norm1":
                        normalize(0, b)
                    elif stage == "energy":
                        row_max(b, i)
                    elif stage == "scale":
                        for n in range(RT):
                            scale_attn(b, n)
                    elif stage == "x":
                        x_low(b, i)
                    elif stage == "attn" and not written_out(b):
                        attn_low(b, i)
                    elif stage == "attn_low":
                        for c in range(KC):
                            attn_low(b, c)
                    elif stage == "mix":
                        add_mix(b, i)
                    elif stage == "stats2":
                        statistics(1, b)
                    elif stage == "norm2":
                        normalize(1, b)
                    elif stage == "h":
                        h_low(b, i)
                    elif stage == "logits":
                        read_logits(b)
                    elif stage == "x_low":
                        scale_attn(b, RT - 1)
                        for c in range(KC):
                            x_low(b, c)
                    elif stage == "logits_before":
                        read_logits(b - 1)
                        route(b - 1)
                    elif stage == "combine":
                        combine_out(b - 1)
                    elif stage == "route":
                        route(b)

            def ffn_block(n, t, b=None):
                def beside(j, point):
                    if b is not None:
                        attention(j, point, b)

                def product(j):
                    dve.wait_ge(up_done, n * UT + j + 1)
                    dve.wait_ge(silu_ready, n * UT + PRIME + j + 1)
                    if j > 1:
                        dve.wait_ge(hid_lo, n * UT + j - 1)
                    nc.vector.tensor_tensor(prod[:, j % 2, :], silu_sb[:, :], up_ps[:, :],
                                            ALU.mult).then_inc(prod_ready, 1)

                def scale(j):
                    dve.wait_ge(prod_ready, n * UT + PRIME + j + 1)
                    for p0, p1, e in pieces[j]:
                        if e not in seen:
                            seen.add(e)
                            dve.wait_ge(combine_loaded[e], n * 16 + 16)
                        for a, z in legal(p0, p1):
                            op = nc.vector.tensor_tensor(prod[a:z, j % 2, :], prod[a:z, j % 2, :],
                                                         combine_b[a:z, e, :], ALU.mult)
                    op.then_inc(scaled, 1)

                def low_part(j):
                    dve.wait_ge(hid_hi, n * UT + j + 1)
                    nc.vector.tensor_tensor(hidden[:, j % 3, LO, :], prod[:, j % 2, :], hidden[:, j % 3, HI, :],
                                            ALU.subtract).then_inc(hid_lo, 1)

                seen = set()
                for j in range(UT):
                    beside(j, "start")
                    beside(j, "gate")
                    product(j)
                    if j == 1:
                        scale(0)
                    if j > 0:
                        scale(j)
                    beside(j, "up")
                    if j == 1:
                        low_part(0)
                    if j > 0:
                        low_part(j)
                    beside(j, "down")
                for i in range(RT):
                    dve.wait_ge(out_done, n * RT + i + 1)
                    nc.vector.tensor_tensor(row_tile(t, i), out_ps[i][:, :], row_tile(t, i),
                                            ALU.add).then_inc(block_summed, 1)

            ffn_block(0, 0, 1)
            with dve.Fori(1, B - 1) as t:
                ffn_block(t, t, t + 1)
            combine_out(B - 1)
            with dve.Fori(B - 1, NG * B) as n:
                ffn_block(n, n % B)

        @block.tensor
        def _(pe):
            def turn_context(b, c):
                if not written_out(b):
                    if c == 0:
                        pe.wait_ge(ctx_loaded, 16 * b)
                    pe.wait_ge((logits_read, combineT_ready)[c], b)
                elif c == 0:
                    pe.wait_ge((ctx_loaded, ctx1_loaded)[b], 16)
                for i in range(RT):
                    op = nc.tensor.transpose(att_bank(b, "ctx", c)[:, i * P:(i + 1) * P],
                                             place(b).ctx_rows[:, i, c * P:(c + 1) * P], ident[:, :])
                op.then_inc(ctx_turned, 1)

            def project(b, i):
                pe.wait_ge(ctxT_ready, CC * b + CC)
                for c in range(CC):
                    op = nc.tensor.matmul(att_bank(b, "qk", i)[:, :], wqkT[:, i, c, :], place(b).ctxT[:, c, :],
                                          start=(c == 0), stop=(c == CC - 1))
                op.then_inc(qk_done, 1)

            def energy(b, n):
                if n == 0:
                    pe.wait_ge(qk_ready, 2 * b + 2)
                elif n >= 2 and not written_out(b):
                    pe.wait_ge(exp_done, RT * b + n - 1)
                nc.tensor.matmul(att_bank(b, "energy", n)[:, :], place(b).qT[:, n * P:(n + 1) * P], place(b).kT,
                                 start=True, stop=True).then_inc(energy_done, 1)

            def turn_x(b, c):
                if c == 0:
                    pe.wait_ge(normed_ready[0], RT * b + RT)
                if written_out(b):
                    pe.wait_ge(exp_done, RT * b + c + 1)
                elif c < 2:
                    pe.wait_ge(exp_done, RT * b + c + 3)
                else:
                    pe.wait_ge(xlo_ready, KC * b + c - 1)
                for i in range(RT):
                    op = nc.tensor.transpose(att_bank(b, "x", c)[:, i * P:(i + 1) * P],
                                             place(b).normed[:, i, c * P:(c + 1) * P], ident[:, :])
                op.then_inc(x_turned, 1)

            def turn_attn(b, c):
                if c == 0:
                    pe.wait_ge(attn_ready, RT * b + RT)
                if written_out(b):
                    pe.wait_ge(xlo_ready, KC * b + c + 1)
                elif c < 2:
                    pe.wait_ge(xlo_ready, KC * b + c + 3)
                else:
                    pe.wait_ge(alo_ready, KC * b + c - 1)
                for m in range(RT):
                    op = nc.tensor.transpose(att_bank(b, "attn", c)[:, m * P:(m + 1) * P],
                                             place(b).expo[:, m, c * P:(c + 1) * P], ident[:, :])
                op.then_inc(attn_turned, 1)

            def mix(b, i):
                if i == 0:
                    pe.wait_ge(xlo_ready, KC * b + KC)
                    if not written_out(b):
                        pe.wait_ge(alo_ready, KC * b + KC)
                elif i >= 2 and not written_out(b):
                    pe.wait_ge(added, RT * b + i - 1)
                for c in range(KC):
                    if i == 0 and written_out(b):
                        pe.wait_ge(alo_ready, KC * b + c + 1)
                    for s, (xp, ap) in enumerate(PAIRS):
                        op = nc.tensor.matmul(att_bank(b, "mix", i)[:, :], place(b).xnT[:, xp, c, i * P:(i + 1) * P],
                                              place(b).attnT[:, ap, c, :], start=(c == 0 and s == 0),
                                              stop=(c == KC - 1 and s == len(PAIRS) - 1))
                op.then_inc(mix_done, 1)

            def turn_h(b, c):
                if c == 0:
                    pe.wait_ge(normed_ready[1], RT * b + RT)
                if c >= 2:
                    pe.wait_ge(hlo_ready, KC * b + c - 1)
                elif written_out(b):
                    pe.wait_ge((logits_read, combineT_ready)[c], b)
                for i in range(RT):
                    op = nc.tensor.transpose(att_bank(b, "h", c)[:, i * P:(i + 1) * P],
                                             place(b).normed[:, i, c * P:(c + 1) * P], ident[:, :])
                op.then_inc(h_turned, 1)

            def turn_h_by_rows(b):
                for i in range(RT):
                    pe.wait_ge(normed_ready[1], RT * b + i + 1)
                    for c in range(KC):
                        op = nc.tensor.transpose(att_bank(b, "h", c)[:, i * P:(i + 1) * P],
                                                 place(b).normed[:, i, c * P:(c + 1) * P], ident[:, :])
                        if i == RT - 1:
                            op.then_inc(h_turned, 1)

            LOGIT_STEPS = KC * RT * 2

            def logits_product(b, k):
                i, c, part = k // (KC * 2), k // 2 % KC, k % 2
                return nc.tensor.matmul(att_bank(b, "logits", 0)[:, i * 3 * NL:(i + 1) * 3 * NL],
                                        hT[:, part, c, bass.ds(b * S + i * P, P)],
                                        gw3[:, c, :, :].rearrange("p a e -> p (a e)"),
                                        start=(c == 0 and part == HI), stop=(c == KC - 1 and part == LO))

            def router_logits(b):
                pe.wait_ge(hlo_ready, KC * b + KC)
                for k in range(LOGIT_STEPS):
                    op = logits_product(b, k)
                op.then_inc(logits_done, 1)

            def turn_combine(b):
                pe.wait_ge(combine_ready, b + 1)
                for i in range(RT):
                    op = nc.tensor.transpose(att_bank(b, "combine", 0)[0:NC, i * P:(i + 1) * P],
                                             combine[:, i, :], ident[:, :])
                op.then_inc(combine_turned, 1)

            pe.wait_ge(consts_ready, 3)
            for _ in range(WARM_UP):
                nc.tensor.transpose(bank[7][:, 0:P], ident[:, :], ident[:, :])
            pe.wait_ge(wqk_loaded, 32)
            for i in range(2):
                for c in range(CC):
                    op = nc.tensor.transpose(bank[4][:, (i * CC + c) * P:(i * CC + c + 1) * P],
                                             wqk[:, i, c * P:(c + 1) * P], ident[:, :])
            op.then_inc(wqk_turned, 1)
            for c in range(CC):
                turn_context(0, c)
            pe.wait_ge(gw_loaded, 32)
            for c in range(KC):
                op = nc.tensor.transpose(bank[5][:, c * NL:(c + 1) * NL], gw_rows[:, c * P:(c + 1) * P],
                                         ident[0:NL, 0:NL])
            op.then_inc(gw_turned, 1)
            pe.wait_ge(wqkT_ready, 1)
            project(0, 0)
            project(0, 1)
            pe.wait_ge(gw_step, 5)
            for c in range(CC):
                turn_context(1, c)
            for n in range(RT):
                energy(0, n)
            turn_x(0, 0)
            turn_x(0, 1)
            project(1, 0)
            turn_x(0, 2)
            turn_x(0, 3)
            project(1, 1)
            for c in range(KC):
                turn_attn(0, c)
            energy(1, 0)
            energy(1, 1)
            for i in range(RT):
                mix(0, i)
            energy(1, 2)
            energy(1, 3)
            turn_x(1, 0)
            turn_x(1, 1)
            turn_h_by_rows(0)
            turn_x(1, 2)
            turn_x(1, 3)

            def attention(j, point, b):
                for stage, i in (AT_POINT_FIRST if written_out(b) else AT_POINT).get((j, point), ()):
                    if stage == "ctx":
                        turn_context(b, i)
                    elif stage == "qk":
                        project(b, i)
                    elif stage == "energy":
                        energy(b, i)
                    elif stage == "x":
                        turn_x(b, i)
                    elif stage == "attn":
                        turn_attn(b, i)
                    elif stage == "mix":
                        mix(b, i)
                    elif stage == "h":
                        turn_h(b, i)
                    elif stage == "logits" and written_out(b):
                        router_logits(b)
                    elif stage == "logits_before":
                        router_logits(b - 1)
                    elif stage == "combine":
                        turn_combine(b - 1)

            def ffn_block(n, g, t, b=None):
                spread = b is not None and not written_out(b)

                def logits_between(first, k):
                    if spread and first is not None and first + k < LOGIT_STEPS:
                        if first + k == 0:
                            pe.wait_ge(hlo_ready, KC * b + KC)
                        op = logits_product(b, first + k)
                        if first + k == LOGIT_STEPS - 1:
                            op.then_inc(logits_done, 1)

                def product(kind, j, ps, logits_from=None):
                    for c in range(KC):
                        if j == 0 and kind == GATE and written_out(b):
                            pe.wait_ge(hlo_ready, c + 1)
                        for s, (wp, hp) in enumerate(PAIRS):
                            op = nc.tensor.matmul(ps[:, :], weights[:, j, wp, kind, c * P:(c + 1) * P],
                                                  hT[:, hp, c, bass.ds(t * S, S)], start=(c == 0 and s == 0),
                                                  stop=(c == KC - 1 and s == len(PAIRS) - 1))
                            if c < KC - 1 or s < len(PAIRS) - 1:
                                logits_between(logits_from, c * len(PAIRS) + s)
                    return op

                def down(j, logits_from=None):
                    pe.wait_ge(hid_lo, n * UT + j + 1)
                    if j == 0:
                        pe.wait_ge(block_summed, n * RT + PRIME)
                        if written_out(b):
                            pe.wait_ge(added, RT * b + RT)
                    for i in range(RT):
                        for s, (hp, wp) in enumerate(PAIRS):
                            op = nc.tensor.matmul(out_ps[i][:, :], hidden[:, j % 3, hp, i * P:(i + 1) * P],
                                                  weights[:, j, wp, DOWN, :], start=(j == 0 and s == 0),
                                                  stop=(j == UT - 1 and s == len(PAIRS) - 1))
                            if i < RT - 1 or s < len(PAIRS) - 1:
                                logits_between(logits_from, i * len(PAIRS) + s)
                        if j == UT - 1:
                            op.then_inc(out_done, 1)
                    if j < UT - 1:
                        op.then_inc(down_done, 1)

                def beside(j, point):
                    if b is not None:
                        attention(j, point, b)

                for j in range(UT):
                    pe.wait_ge(split, g * UT + j + 1)
                    pe.wait_ge(silu_ready, n * UT + PRIME + j)
                    last = j == UT - 1
                    product(GATE, j, gate_ps, 0 if last else None).then_inc(gate_done, 1)
                    beside(j, "gate")
                    pe.wait_ge(prod_ready, n * UT + PRIME + j)
                    product(UP, j, up_ps, 11 if last else None).then_inc(up_done, 1)
                    beside(j, "up")
                    if j >= 2:
                        down(j - 2, 22 if last else None)
                    beside(j, "down")
                for j in range(UT - 2, UT):
                    down(j)

            ffn_block(0, 0, 0, 1)
            with pe.Fori(1, B - 1) as t:
                ffn_block(t, 0, t, t + 1)
            turn_combine(B - 1)
            with pe.Fori(B - 1, NG * B) as n:
                ffn_block(n, n // B, n % B)


_INS = ["x", "ctx_1024", "L0_xattn_Wq", "L0_xattn_bq", "L0_xattn_Wk", "L0_xattn_bk", "L0_ffn_gate_w",
        "L0_ffn_w_gate", "L0_ffn_w_up", "L0_ffn_w_down", "L0_ffn_sw_gate", "L0_ffn_sw_up", "L0_ffn_sw_down",
        "L0_ffn_shared_gate_w"]


def kernel(**inputs):
    import numpy as np
    import concourse.bacc as bacc
    from concourse.bass_utils import run_bass_kernel_spmd

    nc = bacc.Bacc("TRN2", target_bir_lowering=False, num_devices=1)
    arrays, args = {}, []
    for name in _INS:
        a = np.ascontiguousarray(inputs[name])
        arrays[name] = a
        args.append(nc.dram_tensor(name, a.shape, mybir.dt.from_np(a.dtype), kind="ExternalInput").ap())
    shape = inputs["x"].shape
    out = nc.dram_tensor("out", shape, F32, kind="ExternalOutput").ap()
    combine_dram = nc.dram_tensor("combine_dram", (12, shape[0] * shape[1]), F32, kind="Internal").ap()
    build_xattn_moe(nc, *args, out, combine_dram)
    r = run_bass_kernel_spmd(nc, [arrays], core_ids=[0])
    return r.results[0]["out"]
```
